# Optimizing a Trainium2 kernel written in Bass

```python
import numpy as np
import jax
import jax.numpy as jnp

def _softmax(x, axis=-1):
    return jax.nn.softmax(x, axis=axis)

def _gelu(x):
    return jax.nn.gelu(x, approximate=True)

def _silu(x):
    return jax.nn.silu(x)

def _sigmoid(x):
    return jax.nn.sigmoid(x)

def _layernorm(x, axis=-1, eps=1e-05):
    m = jnp.mean(x, axis=axis, keepdims=True)
    v = jnp.var(x, axis=axis, keepdims=True)
    return (x - m) / jnp.sqrt(v + eps)

def _scatter_add(tgt, idx, src, axis=0):
    return tgt.at[idx].add(src)

def _segment_sum(src, seg, n):
    return jax.ops.segment_sum(src, seg, n)
kernel_name = 'mk_adaln_d1_jaxref_r8_7c9596'

def setup_inputs(seed: int=0):
    np.random.seed(seed)
    _w = jnp.asarray

    def _L0_attn_setup():
        import jax, jax.numpy as jnp
        import numpy as np
        D_MODEL = 128
        N_HEADS = 16
        D_HEAD = D_MODEL // N_HEADS
        B, T = (2, 256)
        EPS = 1e-05
        key = jax.random.key(seed)
        ks = jax.random.split(key, 5)
        s = 1.0 / np.sqrt(D_MODEL)
        return {'x': jax.random.normal(ks[0], (B, T, D_MODEL), dtype=jnp.float32), 'W_q': jax.random.normal(ks[1], (D_MODEL, D_MODEL), dtype=jnp.float32) * s, 'W_k': jax.random.normal(ks[2], (D_MODEL, D_MODEL), dtype=jnp.float32) * s, 'W_v': jax.random.normal(ks[3], (D_MODEL, D_MODEL), dtype=jnp.float32) * s, 'W_o': jax.random.normal(ks[4], (D_MODEL, D_MODEL), dtype=jnp.float32) * s, 'gn_weight': jnp.ones((D_MODEL,), dtype=jnp.float32), 'gn_bias': jnp.zeros((D_MODEL,), dtype=jnp.float32)}
    _L0_attn_in = _L0_attn_setup()

    def _L0_ffn_setup():
        import jax, jax.numpy as jnp
        import numpy as np
        B, S, H = (8, 128, 128)
        FF = 512
        E = 8
        TOP_K = 2
        LN_EPS = 1e-12

        def _layernorm(x, w, b):
            mu = jnp.mean(x, axis=-1, keepdims=True)
            var = jnp.mean(jnp.square(x - mu), axis=-1, keepdims=True)
            return (x - mu) * jax.lax.rsqrt(var + LN_EPS) * w + b
        key = jax.random.key(seed)
        ks = jax.random.split(key, 8)
        sc_h = 1.0 / np.sqrt(H)
        sc_ff = 1.0 / np.sqrt(FF)
        return {'hidden_states': jax.random.normal(ks[0], (B, S, H), jnp.float32), 'router_w': jax.random.normal(ks[1], (E, H), jnp.float32) * sc_h, 'router_b': jnp.zeros((E,), jnp.float32), 'w1': jax.random.normal(ks[2], (E, FF, H), jnp.float32) * sc_h, 'b1': jax.random.normal(ks[3], (E, FF), jnp.float32) * 0.01, 'w2': jax.random.normal(ks[4], (E, H, FF), jnp.float32) * sc_ff, 'b2': jax.random.normal(ks[5], (E, H), jnp.float32) * 0.01, 'ln_w': jnp.ones((H,), jnp.float32), 'ln_b': jnp.zeros((H,), jnp.float32)}
    _L0_ffn_in = _L0_ffn_setup()
    _L0_c = _w((lambda *s: np.random.randn(*s).astype(np.float32) * 0.05)(4, 128))
    _L0_wmod = _w((lambda *s: np.random.randn(*s).astype(np.float32) * 0.05)(128, 6 * 128) * 128 ** (-0.5))
    _d = {'L0_attn_x': _L0_attn_in['x'], 'L0_attn_W_q': _L0_attn_in['W_q'], 'L0_attn_W_k': _L0_attn_in['W_k'], 'L0_attn_W_v': _L0_attn_in['W_v'], 'L0_attn_W_o': _L0_attn_in['W_o'], 'L0_attn_gn_weight': _L0_attn_in['gn_weight'], 'L0_attn_gn_bias': _L0_attn_in['gn_bias'], 'L0_ffn_router_w': _L0_ffn_in['router_w'], 'L0_ffn_router_b': _L0_ffn_in['router_b'], 'L0_ffn_w1': _L0_ffn_in['w1'], 'L0_ffn_b1': _L0_ffn_in['b1'], 'L0_ffn_w2': _L0_ffn_in['w2'], 'L0_ffn_b2': _L0_ffn_in['b2'], 'L0_ffn_ln_w': _L0_ffn_in['ln_w'], 'L0_ffn_ln_b': _L0_ffn_in['ln_b'], 'L0_c': _L0_c, 'L0_wmod': _L0_wmod}
    _x0 = _d['L0_attn_x']
    _d['L0_attn_x'] = jax.random.normal(jax.random.fold_in(jax.random.key(seed), 1), (4, 1024, 128), dtype=_x0.dtype)
    del _x0
    return _d

def reference(L0_attn_x, L0_attn_W_q, L0_attn_W_k, L0_attn_W_v, L0_attn_W_o, L0_attn_gn_weight, L0_attn_gn_bias, L0_ffn_router_w, L0_ffn_router_b, L0_ffn_w1, L0_ffn_b1, L0_ffn_w2, L0_ffn_b2, L0_ffn_ln_w, L0_ffn_ln_b, L0_c, L0_wmod):

    def _L0_attn_ref(x, W_q, W_k, W_v, W_o, gn_weight, gn_bias):
        import jax, jax.numpy as jnp
        import numpy as np
        D_MODEL = 128
        N_HEADS = 16
        D_HEAD = D_MODEL // N_HEADS
        B, T = (2, 256)
        EPS = 1e-05
        b, t, dm = x.shape
        h, dh = (N_HEADS, D_HEAD)
        gammas = 1.0 - 2.0 ** (-5.0 - jnp.arange(h, dtype=jnp.float32))
        q = (x @ W_q.T).reshape(b, t, h, dh)
        k = (x @ W_k.T).reshape(b, t, h, dh)
        v = (x @ W_v.T).reshape(b, t, h, dh)
        idx = jnp.arange(t)
        diff = idx[:, None] - idx[None, :]
        pow_ = jnp.maximum(diff, 0).astype(jnp.float32)
        decay = jnp.where(diff >= 0, gammas[:, None, None] ** pow_, 0.0)
        scale = jnp.sqrt(jnp.float32(dh))
        attn = jnp.einsum('bihd,bjhd->bhij', q, k) * decay[None] / scale
        y = jnp.einsum('bhij,bjhd->bihd', attn, v)
        mean = y.mean(axis=(1, 3), keepdims=True)
        var = y.var(axis=(1, 3), keepdims=True)
        yn = (y - mean) / jnp.sqrt(var + EPS)
        yn = yn.reshape(b, t, dm) * gn_weight + gn_bias
        return yn @ W_o.T

    def _L0_ffn_ref(hidden_states, router_w, router_b, w1, b1, w2, b2, ln_w, ln_b):
        import jax, jax.numpy as jnp
        import numpy as np
        B, S, H = (8, 128, 128)
        FF = 512
        E = 8
        TOP_K = 2
        LN_EPS = 1e-12

        def _layernorm(x, w, b):
            mu = jnp.mean(x, axis=-1, keepdims=True)
            var = jnp.mean(jnp.square(x - mu), axis=-1, keepdims=True)
            return (x - mu) * jax.lax.rsqrt(var + LN_EPS) * w + b
        b, s, h = hidden_states.shape
        flat = hidden_states.reshape(-1, h)
        logits = flat @ router_w.T + router_b
        topk_vals, topk_idx = jax.lax.top_k(logits, TOP_K)
        topk_w = jax.nn.softmax(topk_vals, axis=-1)
        out = jnp.zeros_like(flat)
        n_exp = w1.shape[0]
        for e in range(n_exp):
            cw = jnp.sum(jnp.where(topk_idx == e, topk_w, 0.0), axis=-1)
            y = jax.nn.gelu(flat @ w1[e].T + b1[e], approximate=False)
            y = y @ w2[e].T + b2[e]
            out = out + y * cw[:, None]
        out = out.reshape(b, s, h) + hidden_states
        return _layernorm(out, ln_w, ln_b)
    x = L0_attn_x
    mod = (_silu(L0_c) @ L0_wmod).reshape(L0_c.shape[0], 6, 1, -1)
    sa, ca, ga, sb, cb, gb = (mod[:, 0], mod[:, 1], mod[:, 2], mod[:, 3], mod[:, 4], mod[:, 5])
    ga = (2 * (ga >= 0) - 1) * jnp.maximum(jnp.abs(ga), 0.25)
    gb = (2 * (gb >= 0) - 1) * jnp.maximum(jnp.abs(gb), 0.25)
    h = _layernorm(x, axis=-1) * (1 + ca) + sa
    x = x + ga * _L0_attn_ref(h, L0_attn_W_q, L0_attn_W_k, L0_attn_W_v, L0_attn_W_o, L0_attn_gn_weight, L0_attn_gn_bias)
    h = _layernorm(x, axis=-1) * (1 + cb) + sb
    x = x + gb * _L0_ffn_ref(h, L0_ffn_router_w, L0_ffn_router_b, L0_ffn_w1, L0_ffn_b1, L0_ffn_w2, L0_ffn_b2, L0_ffn_ln_w, L0_ffn_ln_b)
    return x

_drawn_inputs = setup_inputs


def setup_inputs(seed=0):
    import zlib

    import numpy as np

    out = dict(_drawn_inputs(seed))
    spreads = {'L0_attn_gn_weight': (1.0, 0.2),
     'L0_attn_gn_bias': (0.0, 0.312),
     'L0_ffn_router_b': (0.0, 0.371),
     'L0_ffn_ln_w': (1.0, 0.2),
     'L0_ffn_ln_b': (0.0, 0.359)}
    factors = {'L0_ffn_b1': 49.789, 'L0_ffn_b2': 34.184}
    for name, (base, spread) in spreads.items():
        noise = np.random.default_rng([zlib.crc32(name.encode()), seed]).standard_normal(out[name].shape)
        drawn = base * np.exp(spread * noise) if base else spread * noise
        out[name] = jnp.asarray(drawn.astype(out[name].dtype))
    for name, factor in factors.items():
        out[name] = (out[name] * factor).astype(out[name].dtype)
    return out
```

```python
from contextlib import ExitStack

import numpy as np

import concourse.bass as bass
from concourse import mybir

F32 = mybir.dt.float32
ACT = mybir.ActivationFunctionType
ALU = mybir.AluOpType
AX = mybir.AxisListType

P = 128
HEADS = 16
DH = P // HEADS
BATCHES = 4
SEQ = 1024
TILES = BATCHES * SEQ // P
TPB = SEQ // P
C = 64
CPT = P // C
GROUPS = 4
HPG = HEADS // GROUPS
EXPERTS = 8
FF = 512
FC = FF // P
TOK = 512
EPS = 1e-5
EPS_FFN = 1e-12


def shape_constants():
    gamma = 1.0 - 2.0 ** (-5.0 - np.arange(HEADS, dtype=np.float64))
    head = np.arange(P) // DH
    j, i = np.arange(C)[:, None], np.arange(C)[None, :]
    decay = np.where(i >= j, gamma[:, None, None] ** np.maximum(i - j, 0), 0.0) / np.sqrt(DH)
    decay = np.tile(decay.transpose(1, 0, 2).reshape(C, HEADS * C), (CPT, 1))
    qdec = np.tile(gamma[head][:, None] ** (np.arange(C)[None, :] + 1) / np.sqrt(DH), (1, CPT))
    kdec = np.zeros((P, CPT, P))
    for c in range(CPT):
        kdec[c * C:(c + 1) * C, c] = gamma[head][None, :] ** (C - 1 - np.arange(C)[:, None])
    same = (head[:, None] == head[None, :]).astype(np.float64)
    n = np.arange(TILES * CPT)
    last = n % (TPB * CPT) == TPB * CPT - 1
    tables = {
        "ident": np.eye(P),
        "same_head": same,
        "head_mean": same / DH,
        "decay": decay,
        "qdec": qdec,
        "kdec": kdec.reshape(P, -1),
        "lane": (np.arange(P)[:, None] % 32 // DH == np.arange(HPG)[None, :]),
        "carry": np.where(last[None, :], 0.0, gamma[head][:, None] ** C),
        "keep": np.tile(1.0 - last[None, CPT - 1::CPT], (P, 1)),
        "rank": np.tile(np.arange(EXPERTS, 0, -1.0)[None, :], (P, 1)),
    }
    return {k: np.ascontiguousarray(v, np.float32) for k, v in tables.items()}


WEIGHTS = [("wqT", P), ("wkT", P), ("wvT", P), ("wkT2", P), ("woT", P), ("wmod", 6 * P), ("cT", BATCHES),
           ("gn_w", 1), ("gn_b", 1), ("rwT", EXPERTS), ("r_b", EXPERTS), ("ln_w", P), ("ln_b", P)]
EXPERT_COLS = FF + FC * P + FC


def offsets(widths):
    at, out = 0, {}
    for name, n in widths:
        out[name] = (at, at + n)
        at += n
    return out, at


def build(nc, x, weights, consts, experts, b2, out):
    const_at, const_cols = offsets([(k, v.shape[1]) for k, v in shape_constants().items()])
    weight_at, weight_cols = offsets(WEIGHTS)

    with ExitStack() as ctx:
        def sb(name, cols, parts=P):
            return ctx.enter_context(nc.sbuf_tensor(name, [parts, cols], F32))

        def sem(name):
            return ctx.enter_context(nc.semaphore(name))

        CONST = sb("CONST", const_cols)
        WGT = sb("WGT", weight_cols)

        def const(name):
            return CONST[:, const_at[name][0]:const_at[name][1]]

        def wgt(name):
            return WGT[:, weight_at[name][0]:weight_at[name][1]]

        X = sb("X", TILES * P)
        YT = sb("YT", TILES * P)
        H2T = sb("H2T", TILES * P)
        H2 = sb("H2", TILES * P)
        CW = sb("CW", TILES * EXPERTS)
        stat = sb("stat", TILES * 6)
        ystat = sb("ystat", TILES * 6)
        xstat = sb("xstat", TILES * 6)
        mean1, rstd1 = sb("mean1", TILES), sb("rstd1", TILES)
        mean2, rstd2 = sb("mean2", TILES), sb("rstd2", TILES)
        var = sb("var", TILES)
        half = sb("half", TILES)
        minus_half = sb("minus_half", TILES)
        silu = sb("silu", 3 * BATCHES)
        silu_bc = sb("silu_bc", BATCHES * P)
        shiftT, scaleT = sb("shiftT", TILES), sb("scaleT", TILES)
        MOD = sb("MOD", BATCHES * 4 * P)
        gate = sb("gate", 2 * BATCHES * P)
        WOG = sb("WOG", BATCHES * P)
        LNW, LNB = sb("LNW", BATCHES * P), sb("LNB", BATCHES * P)
        gn = sb("gn", 2 * BATCHES)
        gsc = sb("gsc", 4 * BATCHES)
        ga_t, gb_t = sb("gn_scale", TILES), sb("gn_shift", TILES)

        h0 = [sb(f"h0_{p}", P) for p in range(2)]
        hT = [sb(f"hT_{p}", P) for p in range(2)]
        qS = [sb(f"qS_{p}", P) for p in range(2)]
        Qm = [sb(f"Qm_{p}", HPG * P) for p in range(2)]
        KV = [sb(f"KV_{p}", 2 * P) for p in range(2)]
        Kd = [sb(f"Kd_{p}", CPT * P) for p in range(2)]
        Qd = [sb(f"Qd_{p}", P) for p in range(2)]
        PR = [sb(f"PR_{p}", HEADS * C) for p in range(2)]
        ySB = [sb(f"ySB_{p}", P) for p in range(2)]
        UM = sb("UM", CPT * P)
        STATE = [sb(f"STATE_{n}", P) for n in range(4)]
        yn = [sb(f"yn_{p}", P) for p in range(2)]
        hh = [sb(f"hh_{p}", 2 * P) for p in range(2)]
        h2t = [sb(f"h2t_{p}", P) for p in range(2)]
        route = sb("route", 8 * TILES * EXPERTS)
        topv = sb("topv", 4 * TILES)
        EW = [sb(f"EW_{p}", EXPERT_COLS) for p in range(2)]
        EB2 = [sb(f"EB2_{p}", P, 1) for p in range(2)]
        ones = sb("ones", P, 1)
        HID = [sb(f"HID_{f}", TOK) for f in range(FC)]
        fin = [sb(f"fin_{p}", P) for p in range(2)]
        fstat = sb("fstat", TILES * 6)

        bank = [ctx.enter_context(nc.psum_tensor(f"bank{n}", [P, 512], F32)) for n in range(8)]
        TB, QB, KB, YB = bank[0], bank[1], bank[2], bank[3]
        SC = bank[4:8]

        x_loaded = [sem(f"x_loaded{b}") for b in range(BATCHES)]
        const_loaded, wgt_loaded = sem("const_loaded"), sem("wgt_loaded")
        dve_chain, act_step, pool_step, silu_ready = sem("dve_chain"), sem("act_step"), sem("pool_step"), sem("silu_ready")
        stat_ready, h2_kept, fin_c = sem("stat_ready"), sem("h2_kept"), sem("fin_c")
        var_ready, rstd_ready = sem("var_ready"), sem("rstd_ready")
        mod_ready, mod_read = sem("mod_ready"), sem("mod_read")
        h0_ready, h0T_ready, hT_ready = sem("h0_ready"), sem("h0T_ready"), sem("hT_ready")
        q_ready, kv_ready, qm_ready = sem("q_ready"), sem("kv_ready"), sem("qm_ready")
        kvs_ready, qd_ready = sem("kvs_ready"), sem("qd_ready")
        sc_ready, p_ready = sem("sc_ready"), sem("p_ready")
        u_ready, um_ready, s_ready = sem("u_ready"), sem("um_ready"), sem("s_ready")
        y_ready, ysb_ready, yT_ready, YT_ready = sem("y_ready"), sem("ysb_ready"), sem("yT_ready"), sem("YT_ready")
        ystat_ready = sem("ystat_ready")
        gmean_ready, gn_ready = sem("gmean_ready"), sem("gn_ready")
        yn_ready, att_ready, x2_ready = sem("yn_ready"), sem("att_ready"), sem("x2_ready")
        xstat_ready = sem("xstat_ready")
        n2_ready, m2_ready, h2_ready = sem("n2_ready"), sem("m2_ready"), sem("h2_ready")
        h2T_ready, H2T_ready, lg_ready, logit_ready = sem("h2T_ready"), sem("H2T_ready"), sem("lg_ready"), sem("logit_ready")
        exp_ready, cw_ready = sem("exp_ready"), sem("cw_ready")
        ew_loaded = [sem(f"ew_loaded{p}") for p in range(2)]
        hid_ps, hid_ready, moe_ready, moe_added = sem("hid_ps"), sem("hid_ready"), sem("moe_ready"), sem("moe_added")
        fstat_ready, fin_ready = sem("fstat_ready"), sem("fin_ready")
        fin_a, fin_b = sem("fin_a"), sem("fin_b")
        stored = [sem(f"stored{p}") for p in range(2)]

        block = ctx.enter_context(nc.Block())

        def need(eng, s, value):
            if isinstance(value, int) and value <= 0:
                return
            eng.wait_ge(s, value)

        def tile_loop(eng, step):
            step(0, 0)
            step(1, 1)
            with eng.Fori(1, TILES // 2 - 1) as pair:
                step(2 * pair, 0)
                step(2 * pair + 1, 1)
            step(TILES - 2, 0)
            step(TILES - 1, 1)

        def cols(tensor, t, n=P):
            return tensor[:, t * n:(t + 1) * n] if isinstance(t, int) else tensor[:, bass.ds(t * n, n)]

        def last_tile(t):
            return isinstance(t, int) and t == TILES - 1

        def first_tile(t):
            return isinstance(t, int) and t == 0

        @block.sync
        def _(sp):
            x_v = x.rearrange("b (n p) d -> p b n d", p=P)
            for b in range(BATCHES):
                sp.dma_start(X[:, b * SEQ:(b + 1) * SEQ].rearrange("p (n d) -> p n d", d=P), x_v[:, b])\
                  .then_inc(x_loaded[b], 16)
                if b == 0:
                    sp.dma_start(WGT[:, :], weights).then_inc(wgt_loaded, 16)
                    sp.dma_start(CONST[:, :], consts).then_inc(const_loaded, 16)

            def load_expert(e, p):
                sp.dma_start(EW[p][:, :], experts[bass.ds(e, 1)].rearrange("a p n -> p (a n)"))\
                  .then_inc(ew_loaded[p], 16)
                sp.dma_start(EB2[p][:, :], b2[bass.ds(e, 1), :]).then_inc(ew_loaded[p], 16)

            load_expert(0, 0)
            load_expert(1, 1)
            with sp.Fori(1, EXPERTS // 2) as pair:
                for p in range(2):
                    e = 2 * pair
                    sp.wait_ge(moe_ready, (e + p - 1) * (TILES * P // TOK))
                    load_expert(e + p, p)

            out_v = out.rearrange("b (n p) d -> (b n) p d", p=P)

            def store(t, p):
                need(sp, fin_ready, t + 1)
                sp.dma_start(out_v[t] if isinstance(t, int) else out_v[bass.ds(t, 1)].rearrange("a p d -> (a p) d"),
                             fin[p][:, :]).then_inc(stored[p], 16)

            tile_loop(sp, store)
            for p in range(2):
                sp.wait_ge(stored[p], 16 * TILES // 2)

        @block.gpsimd
        def _(pool):
            nc.gpsimd.memset(minus_half[:, :], -0.5).then_inc(pool_step, 1)
            nc.gpsimd.memset(STATE[0][:, :], 0.0).then_inc(pool_step, 1)
            nc.gpsimd.memset(ones[:, :], 1.0).then_inc(pool_step, 1)
            pool.wait_ge(pool_step, 3)
            step = [0]

            def rsqrt(dst, src):
                step[0] += 1
                pool.wait_ge(var_ready, step[0])
                n = dst.shape[1]
                nc.gpsimd.tensor_tensor(dst, src, minus_half[:, 0:n], ALU.pow).then_inc(rstd_ready, 1)

            for b in range(BATCHES):
                rsqrt(rstd1[:, b * TPB:(b + 1) * TPB], var[:, b * TPB:(b + 1) * TPB])
            rsqrt(gsc[:, 0:BATCHES], gsc[:, BATCHES:2 * BATCHES])
            rsqrt(rstd2[:, :], var[:, :])
            rsqrt(rstd1[:, :], var[:, :])

        @block.scalar
        def _(act):
            act.wait_ge(wgt_loaded, 16)
            nc.scalar.activation(silu[:, 0:BATCHES], wgt("cT"), ACT.Exp, scale=-1.0).then_inc(act_step, 1)

            def front(u, p):
                need(act, h0T_ready, u + 1)
                need(act, kv_ready, u - 1)
                nc.scalar.activation(hT[p][:, :], TB[:, 0:P], ACT.Identity, bias=cols(shiftT, u, 1),
                                     scale=cols(scaleT, u, 1)).then_inc(hT_ready, 1)

            def queries(u, p):
                need(act, q_ready, u + 1)
                need(act, qd_ready, u - 1)
                nc.scalar.activation(qS[p][:, :], QB[:, 0:P], ACT.Copy)
                need(act, sc_ready, 4 * (u - 1))
                for a in range(HPG):
                    dst = Qm[p][:, :].rearrange("q (c a i) -> q c a i", c=CPT, a=HPG)[:, :, a, :]
                    last = nc.scalar.activation(dst, QB[:, 0:P].rearrange("q (c i) -> q c i", c=CPT), ACT.Copy,
                                                scale=const("lane")[:, a:a + 1])
                last.then_inc(qm_ready, 1)

            def y_back(t):
                need(act, yT_ready, t + 1)
                nc.scalar.activation(cols(YT, t), TB[:, 0:P], ACT.Copy).then_inc(YT_ready, 1)

            def step(t, p):
                if not last_tile(t):
                    front(t + 1, 1 - p)
                if not first_tile(t):
                    y_back(t - 1)
                if not last_tile(t):
                    queries(t + 1, 1 - p)

            act.wait_ge(const_loaded, 16)
            act.wait_ge(mod_read, 2)
            front(0, 0)
            queries(0, 0)
            tile_loop(act, step)
            y_back(TILES - 1)

            act.wait_ge(gn_ready, 1)
            act.wait_ge(YT_ready, TILES)

            def norm_y(t, p):
                need(act, att_ready, t - 1)
                nc.scalar.activation(yn[p][:, :], cols(YT, t), ACT.Identity, bias=cols(gb_t, t, 1),
                                     scale=cols(ga_t, t, 1)).then_inc(yn_ready, 1)

            tile_loop(act, norm_y)

            def h2_back(t, p):
                need(act, h2T_ready, t + 1)
                need(act, lg_ready, t - 1)
                nc.scalar.activation(cols(H2T, t), bank[4 + p][:, 0:P], ACT.Copy)
                nc.scalar.activation(h2t[p][:, :], bank[4 + p][:, 0:P], ACT.Copy).then_inc(H2T_ready, 1)

            tile_loop(act, h2_back)
            act.wait_ge(exp_ready, 1)
            nc.scalar.activation(topv[:, 3 * TILES:4 * TILES], topv[:, 2 * TILES:3 * TILES], ACT.Exp).then_inc(exp_ready, 1)

            def gelu(k, p):
                for f in range(FC):
                    act.wait_ge(hid_ps, k * FC + f + 1)
                    if f == 0:
                        need(act, moe_ready, k)
                    nc.scalar.activation(HID[f][:, :], bank[f % 2][:, :], ACT.Gelu,
                                         bias=EW[p][:, FF + FC * P + f:FF + FC * P + f + 1]).then_inc(hid_ready, 1)

            STEPS = TILES * P // TOK
            gelu(0, 0)
            with act.Fori(1, STEPS) as s:
                gelu(s, 0)
            with act.Fori(STEPS, 2 * STEPS) as s:
                gelu(s, 1)
            with act.Fori(1, EXPERTS // 2) as pair:
                for p in range(2):
                    e = 2 * pair
                    with act.Fori(0, STEPS) as s:
                        gelu((e + p) * STEPS + s, p)

        @block.tensor
        def _(pe):
            mm = nc.tensor.matmul
            pe.wait_ge(wgt_loaded, 16)
            pe.wait_ge(silu_ready, 1)
            for n in range(2):
                mm(bank[4][:, n * BATCHES:(n + 1) * BATCHES], wgt("wmod")[:, n * P:(n + 1) * P],
                   silu[:, 2 * BATCHES:3 * BATCHES], start=True, stop=True, skip_group_check=True)\
                    .then_inc(mod_ready, 1)
            for b in range(BATCHES):
                mm(bank[b][:, :], cols(silu_bc, b), wgt("wmod")[:, 2 * P:6 * P],
                   start=True, stop=True).then_inc(mod_ready, 1)

            def transpose_in(u, p):
                need(pe, h0_ready, u + 1)
                need(pe, YT_ready, u - 2)
                if isinstance(u, int) and u == 1:
                    pe.wait_ge(hT_ready, 1)
                nc.tensor.transpose(TB[:, 0:P], h0[p][:, :], const("ident")).then_inc(h0T_ready, 1)

            def project(u, p):
                need(pe, hT_ready, u + 1)
                need(pe, qm_ready, u)
                mm(QB[:, 0:P], wgt("wqT"), hT[p][:, :], start=True, stop=True).then_inc(q_ready, 1)
                need(pe, kvs_ready, u)
                mm(KB[:, 0:P], wgt("wkT"), hT[p][:, :], start=True, stop=True)
                mm(KB[:, P:3 * P], hT[p][:, :], WGT[:, weight_at["wvT"][0]:weight_at["wkT2"][1]],
                   start=True, stop=True, skip_group_check=True).then_inc(kv_ready, 1)

            def scores(t, p):
                need(pe, qm_ready, t + 1)
                need(pe, kvs_ready, t + 1)
                for g in range(GROUPS):
                    need(pe, p_ready, GROUPS * (t - 1) + g + 1)
                    rows = slice(32 * g, 32 * g + 32)
                    for c in range(CPT):
                        last = mm(SC[g][c * C:(c + 1) * C, 0:HPG * C], KV[p][rows, c * C:(c + 1) * C],
                                  Qm[p][rows, c * HPG * C:(c + 1) * HPG * C], start=True, stop=True)
                    last.then_inc(sc_ready, 1)

            def y_transpose(t, p):
                need(pe, ysb_ready, t + 1)
                need(pe, hT_ready, min(t + 3, TILES) if isinstance(t, int) else t + 3)
                nc.tensor.transpose(TB[:, 0:P], ySB[p][:, :], const("ident")).then_inc(yT_ready, 1)

            def state_updates(t, p):
                need(pe, ysb_ready, t)
                for c in range(CPT):
                    last = mm(YB[:, (1 + c) * P:(2 + c) * P], Kd[p][:, c * P:(c + 1) * P], KV[p][:, P:2 * P],
                              start=True, stop=True, skip_group_check=True)
                last.then_inc(u_ready, 1)

            def outputs(t, p):
                need(pe, um_ready, 2 * t + 2)
                need(pe, qd_ready, t + 1)
                need(pe, p_ready, GROUPS * (t + 1))
                need(pe, s_ready, 2 * t + 1)
                for c in range(CPT):
                    mm(YB[c * C:(c + 1) * C, 0:P], Qd[p][:, c * C:(c + 1) * C], STATE[(2 * p + c) % 4][:, :],
                       start=True, stop=False, skip_group_check=True)
                for h in range(HEADS):
                    for c in range(CPT):
                        rows = slice(c * C, (c + 1) * C)
                        last = mm(YB[rows, h * DH:(h + 1) * DH], PR[p][rows, h * C:(h + 1) * C],
                                  KV[p][rows, P + h * DH:P + (h + 1) * DH], start=False, stop=True,
                                  skip_group_check=True)
                last.then_inc(y_ready, 1)

            def step(t, p):
                if not last_tile(t):
                    transpose_in(t + 1, 1 - p)
                scores(t, p)
                if not first_tile(t):
                    y_transpose(t - 1, 1 - p)
                if not last_tile(t):
                    project(t + 1, 1 - p)
                state_updates(t, p)
                outputs(t, p)

            pe.wait_ge(const_loaded, 16)
            pe.wait_ge(mod_read, 2 + BATCHES)
            transpose_in(0, 0)
            project(0, 0)
            pe.wait_ge(pool_step, 3)
            tile_loop(pe, step)
            y_transpose(TILES - 1, 1)

            pe.wait_ge(gmean_ready, 1)
            mm(bank[4][:, 0:2 * BATCHES], const("head_mean"), gn[:, :], start=True, stop=True).then_inc(gmean_ready, 1)

            def attend(t, p):
                need(pe, yn_ready, t + 1)
                need(pe, x2_ready, t - 1)
                b = t // TPB
                mm(bank[6 + p][:, 0:P], yn[p][:, :], cols(WOG, b), start=True, stop=True).then_inc(att_ready, 1)

            tile_loop(pe, attend)

            def h2_transpose(t, p):
                need(pe, h2_ready, t + 1)
                need(pe, H2T_ready, t - 1)
                nc.tensor.transpose(bank[4 + p][:, 0:P], hh[p][:, P:2 * P], const("ident")).then_inc(h2T_ready, 1)

            def logits(t, p):
                need(pe, H2T_ready, t + 1)
                mm(cols(bank[2], t, EXPERTS), h2t[p][:, :], wgt("rwT"), start=True, stop=True,
                   skip_group_check=True).then_inc(lg_ready, 1)

            def b_step(t, p):
                h2_transpose(t, p)
                if not first_tile(t):
                    logits(t - 1, 1 - p)

            tile_loop(pe, b_step)
            logits(TILES - 1, 1)

            pe.wait_ge(cw_ready, 1)

            def expert_step(k, s, p):
                for f in range(FC):
                    need(pe, hid_ready, k * FC + f - 1)
                    mm(bank[f % 2][:, :], EW[p][:, f * P:(f + 1) * P], cols(H2T, s, TOK), start=True, stop=True)\
                        .then_inc(hid_ps, 1)
                need(pe, hid_ready, (k + 1) * FC)
                need(pe, moe_added, k)
                for n in range(TOK // P):
                    mm(bank[3][:, n * P:(n + 1) * P], ones[:, :], EB2[p][:, :], start=True, stop=False,
                       skip_group_check=True)
                    for f in range(FC):
                        last = mm(bank[3][:, n * P:(n + 1) * P], HID[f][:, n * P:(n + 1) * P],
                                  EW[p][:, FF + f * P:FF + (f + 1) * P], start=False, stop=(f == FC - 1),
                                  skip_group_check=True)
                last.then_inc(moe_ready, 1)

            STEPS = TILES * P // TOK
            pe.wait_ge(ew_loaded[0], 32)
            expert_step(0, 0, 0)
            with pe.Fori(1, STEPS) as s:
                expert_step(s, s, 0)
            pe.wait_ge(ew_loaded[1], 32)
            with pe.Fori(0, STEPS) as s:
                expert_step(STEPS + s, s, 1)
            with pe.Fori(1, EXPERTS // 2) as pair:
                for p in range(2):
                    e = 2 * pair
                    with pe.Fori(0, STEPS) as s:
                        pe.wait_ge(ew_loaded[p], (pair + 1) * 32)
                        expert_step((e + p) * STEPS + s, s, p)

        @block.vector
        def _(dve):
            v = nc.vector
            chain = [0]

            def link(ins):
                chain[0] += 1
                ins.then_inc(dve_chain, 1)
                dve.wait_ge(dve_chain, chain[0])

            def moments(stats, mean, variance, tmp, eps):
                s = stats.rearrange("p (t s) -> p t s", s=6)
                link(v.tensor_tensor(tmp, s[:, :, 1], s[:, :, 4], ALU.subtract))
                link(v.tensor_tensor(mean, s[:, :, 1], s[:, :, 4], ALU.add))
                link(v.tensor_scalar(mean, mean, 0.5, None, ALU.mult))
                link(v.tensor_tensor(tmp, tmp, tmp, ALU.mult))
                link(v.tensor_tensor(variance, s[:, :, 2], s[:, :, 5], ALU.add))
                link(v.tensor_scalar(variance, variance, 1.0 / P, eps, ALU.mult, ALU.add))
                v.scalar_tensor_tensor(out=variance, in0=tmp, scalar=0.25, in1=variance, op0=ALU.mult,
                                       op1=ALU.add).then_inc(var_ready, 1)

            def per_batch(ap):
                return ap.unsqueeze(2).broadcast_to((P, BATCHES, TPB))

            dve.wait_ge(act_step, 1)
            link(v.tensor_scalar(silu[:, 0:BATCHES], silu[:, 0:BATCHES], 1.0, None, ALU.add))
            link(v.reciprocal(silu[:, BATCHES:2 * BATCHES], silu[:, 0:BATCHES]))
            link(v.tensor_tensor(silu[:, 2 * BATCHES:3 * BATCHES], silu[:, BATCHES:2 * BATCHES], wgt("cT"), ALU.mult))
            v.tensor_copy(silu_bc[:, :].rearrange("p (b m) -> p b m", b=BATCHES),
                          silu[:, 2 * BATCHES:3 * BATCHES].unsqueeze(2).broadcast_to((P, BATCHES, P)))\
             .then_inc(silu_ready, 1)

            for b in range(BATCHES):
                dve.wait_ge(x_loaded[b], 16)
                with dve.Fori(b * TPB, (b + 1) * TPB) as t:
                    v.bn_stats(cols(stat, t, 6), cols(X, t)).then_inc(stat_ready, 1)
                dve.wait_ge(stat_ready, (b + 1) * TPB)
                at = slice(b * TPB, (b + 1) * TPB)
                moments(stat[:, b * TPB * 6:(b + 1) * TPB * 6], mean1[:, at], var[:, at], half[:, at], EPS)

            dve.wait_ge(mod_ready, 2)
            sa, ca = bank[4][:, 0:BATCHES], bank[4][:, BATCHES:2 * BATCHES]
            v.tensor_copy(shiftT[:, :].rearrange("p (b t) -> p b t", b=BATCHES), per_batch(sa)).then_inc(mod_read, 1)
            v.tensor_scalar(scaleT[:, :].rearrange("p (b t) -> p b t", b=BATCHES), per_batch(ca), 1.0, None,
                            ALU.add).then_inc(mod_read, 1)
            for b in range(BATCHES):
                dve.wait_ge(mod_ready, 3 + b)
                v.tensor_copy(MOD[:, b * 4 * P:(b + 1) * 4 * P], bank[b][:, :]).then_inc(mod_read, 1)
            dve.wait_ge(mod_read, 2 + BATCHES)
            mod = MOD[:, :].rearrange("p (b k d) -> p b k d", b=BATCHES, k=4)
            three = lambda tensor: tensor[:, 0:BATCHES * P].rearrange("p (b d) -> p b d", b=BATCHES)
            spread = lambda ap: ap.unsqueeze(1).broadcast_to((P, BATCHES, P))

            def clamp_gate(k):
                g = mod[:, :, k, :]
                hi = gate[:, BATCHES * P:].rearrange("p (b d) -> p b d", b=BATCHES)
                link(v.scalar_tensor_tensor(out=hi, in0=g, scalar=-1.0, in1=g, op0=ALU.mult, op1=ALU.max))
                link(v.tensor_scalar(hi, hi, 0.25, None, ALU.max))
                link(v.tensor_scalar(three(gate), g, 0.0, 2.0, ALU.is_ge, ALU.mult))
                link(v.scalar_tensor_tensor(out=gate[:, 0:BATCHES * P], in0=gate[:, 0:BATCHES * P], scalar=-1.0,
                                            in1=gate[:, BATCHES * P:], op0=ALU.add, op1=ALU.mult))

            clamp_gate(0)
            link(v.tensor_tensor(three(WOG), three(gate), spread(wgt("woT")), ALU.mult))
            clamp_gate(3)
            link(v.tensor_tensor(three(LNW), three(gate), spread(wgt("ln_w")), ALU.mult))
            link(v.tensor_tensor(three(LNB), three(gate), spread(wgt("ln_b")), ALU.mult))
            link(v.tensor_scalar(mod[:, :, 2, :], mod[:, :, 2, :], 1.0, None, ALU.add))

            def normalise(u, p):
                need(dve, h0T_ready, u - 1)
                v.tensor_scalar(h0[p][:, :], cols(X, u), cols(mean1, u, 1), cols(rstd1, u, 1), ALU.subtract,
                                ALU.mult).then_inc(h0_ready, 1)

            def keys_values(u, p):
                need(dve, y_ready, u - 1)
                need(dve, kv_ready, u + 1)
                v.tensor_copy(KV[p][:, :], KB[:, 0:2 * P])
                v.tensor_tensor(Kd[p][:, :].rearrange("q (c d) -> q c d", c=CPT),
                                KB[:, 2 * P:3 * P].unsqueeze(1).broadcast_to((P, CPT, P)),
                                const("kdec").rearrange("q (c d) -> q c d", c=CPT), ALU.mult).then_inc(kvs_ready, 1)
                need(dve, qm_ready, u + 1)
                v.tensor_tensor(Qd[p][:, :], qS[p][:, :], const("qdec"), ALU.mult).then_inc(qd_ready, 1)

            def mask(t, p):
                for g in range(GROUPS):
                    need(dve, sc_ready, GROUPS * t + g + 1)
                    at = slice(g * HPG * C, (g + 1) * HPG * C)
                    v.tensor_tensor(PR[p][:, at], SC[g][:, 0:HPG * C], const("decay")[:, at], ALU.mult)\
                     .then_inc(p_ready, 1)

            def y_out(t, p):
                need(dve, yT_ready, t - 1)
                need(dve, y_ready, t + 1)
                v.tensor_copy(ySB[p][:, :], YB[:, 0:P]).then_inc(ysb_ready, 1)

            def states(t, p):
                need(dve, u_ready, t + 1)
                v.tensor_tensor(UM[:, 0:P], YB[:, P:2 * P], const("same_head"), ALU.mult).then_inc(um_ready, 1)
                v.scalar_tensor_tensor(out=UM[:, P:2 * P], in0=YB[:, 2 * P:3 * P], scalar=cols(const("keep"), t, 1),
                                       in1=const("same_head"), op0=ALU.mult, op1=ALU.mult).then_inc(um_ready, 1)
                for c in range(CPT):
                    if c == 0:
                        need(dve, um_ready, 2 * t + 2)
                    else:
                        need(dve, s_ready, 2 * t + 1)
                    v.scalar_tensor_tensor(out=STATE[(2 * p + c + 1) % 4][:, :], in0=STATE[(2 * p + c) % 4][:, :],
                                           scalar=cols(const("carry"), 2 * t + c, 1), in1=UM[:, c * P:(c + 1) * P],
                                           op0=ALU.mult, op1=ALU.add).then_inc(s_ready, 1)

            def y_stats(t):
                v.bn_stats(cols(ystat, t, 6), cols(YT, t)).then_inc(ystat_ready, 1)

            def step(t, p):
                if not last_tile(t):
                    normalise(t + 1, 1 - p)
                if not first_tile(t):
                    y_out(t - 1, 1 - p)
                mask(t, p)
                if not first_tile(t):
                    need(dve, YT_ready, t)
                if not last_tile(t):
                    keys_values(t + 1, 1 - p)
                if not first_tile(t):
                    y_stats(t - 1)
                need(dve, s_ready, 2 * t)
                states(t, p)

            dve.wait_ge(rstd_ready, BATCHES)
            dve.wait_ge(pool_step, 3)
            normalise(0, 0)
            keys_values(0, 0)
            tile_loop(dve, step)
            y_out(TILES - 1, 1)
            dve.wait_ge(YT_ready, TILES)
            y_stats(TILES - 1)

            dve.wait_ge(ystat_ready, TILES)
            ys = ystat[:, :].rearrange("p (b n s) -> p b n s", b=BATCHES, s=3)
            mu, m2 = ys[:, :, :, 1], ys[:, :, :, 2]
            mean_c, square_c = gn[:, 0:BATCHES], gn[:, BATCHES:]
            sq = stat[:, 0:2 * TILES].rearrange("p (b n) -> p b n", b=BATCHES)
            link(v.tensor_reduce(mean_c, mu, AX.X, ALU.add))
            link(v.tensor_scalar(mean_c, mean_c, 1.0 / (2 * TPB), None, ALU.mult))
            link(v.tensor_tensor(sq, mu, mu, ALU.mult))
            link(v.tensor_scalar(sq, sq, P / 2.0, None, ALU.mult))
            link(v.tensor_tensor(sq, sq, m2, ALU.add))
            link(v.tensor_reduce(square_c, sq, AX.X, ALU.add))
            v.tensor_scalar(square_c, square_c, 1.0 / SEQ, None, ALU.mult).then_inc(gmean_ready, 1)
            dve.wait_ge(gmean_ready, 2)
            mean_h, square_h = gsc[:, 2 * BATCHES:3 * BATCHES], gsc[:, 3 * BATCHES:]
            var_h, rstd_h = gsc[:, BATCHES:2 * BATCHES], gsc[:, 0:BATCHES]
            link(v.tensor_copy(gsc[:, 2 * BATCHES:], bank[4][:, 0:2 * BATCHES]))
            link(v.tensor_tensor(var_h, mean_h, mean_h, ALU.mult))
            link(v.tensor_tensor(var_h, square_h, var_h, ALU.subtract))
            v.tensor_scalar(var_h, var_h, EPS, None, ALU.add).then_inc(var_ready, 1)
            dve.wait_ge(rstd_ready, BATCHES + 1)
            link(v.tensor_scalar(rstd_h, rstd_h, wgt("gn_w"), None, ALU.mult))
            link(v.tensor_tensor(mean_h, mean_h, rstd_h, ALU.mult))
            link(v.tensor_scalar(mean_h, mean_h, -1.0, wgt("gn_b"), ALU.mult, ALU.add))
            link(v.tensor_copy(ga_t[:, :].rearrange("p (b t) -> p b t", b=BATCHES), per_batch(rstd_h)))
            v.tensor_copy(gb_t[:, :].rearrange("p (b t) -> p b t", b=BATCHES), per_batch(mean_h)).then_inc(gn_ready, 1)

            def residual(t, p):
                need(dve, att_ready, t + 1)
                v.tensor_tensor(cols(X, t), bank[6 + p][:, 0:P], cols(X, t), ALU.add).then_inc(x2_ready, 1)

            tile_loop(dve, residual)
            dve.wait_ge(x2_ready, TILES)
            with dve.Fori(0, TILES) as t:
                v.bn_stats(cols(xstat, t, 6), cols(X, t)).then_inc(xstat_ready, 1)
            dve.wait_ge(xstat_ready, TILES)
            moments(xstat[:, :], mean2[:, :], var[:, :], half[:, :], EPS)
            dve.wait_ge(rstd_ready, BATCHES + 2)

            def hidden(t, p):
                b = t // TPB
                need(dve, h2T_ready, t - 1)
                v.tensor_scalar(hh[p][:, 0:P], cols(X, t), cols(mean2, t, 1), cols(rstd2, t, 1), ALU.subtract,
                                ALU.mult).then_inc(n2_ready, 1)
                need(dve, n2_ready, t + 1)
                v.tensor_tensor(hh[p][:, 0:P], hh[p][:, 0:P], cols(MOD, 4 * b + 2), ALU.mult).then_inc(m2_ready, 1)
                need(dve, m2_ready, t + 1)
                v.tensor_tensor(hh[p][:, P:2 * P], hh[p][:, 0:P], cols(MOD, 4 * b + 1), ALU.add).then_inc(h2_ready, 1)
                need(dve, h2_ready, t + 1)
                v.tensor_copy(cols(H2, t), hh[p][:, P:2 * P]).then_inc(h2_kept, 1)

            tile_loop(dve, hidden)

            dve.wait_ge(lg_ready, TILES)
            dve.wait_ge(h2_kept, TILES)
            TE = TILES * EXPERTS
            te = lambda n: route[:, n * TE:(n + 1) * TE].rearrange("p (t e) -> p t e", e=EXPERTS)
            over = lambda ap: ap.unsqueeze(1).broadcast_to((P, TILES, EXPERTS))
            per_tile = lambda n: topv[:, n * TILES:(n + 1) * TILES]
            wide = lambda ap: ap.unsqueeze(2).broadcast_to((P, TILES, EXPERTS))
            link(v.tensor_tensor(te(0), bank[2][:, 0:TE].rearrange("p (t e) -> p t e", e=EXPERTS), over(wgt("r_b")), ALU.add))

            def first_of_largest(logits, value, onehot):
                link(v.tensor_reduce(value, logits, AX.X, ALU.max))
                link(v.tensor_tensor(onehot, logits, wide(value), ALU.is_equal))
                link(v.tensor_tensor(onehot, onehot, over(const("rank")), ALU.mult))
                link(v.tensor_reduce(per_tile(2), onehot, AX.X, ALU.max))
                link(v.tensor_tensor(onehot, over(const("rank")), wide(per_tile(2)), ALU.is_equal))

            first_of_largest(te(0), per_tile(0), te(1))
            link(v.tensor_scalar(te(2), te(1), -3.0e38, None, ALU.mult))
            link(v.tensor_tensor(te(2), te(2), te(0), ALU.add))
            first_of_largest(te(2), per_tile(1), te(3))
            v.tensor_tensor(per_tile(2), per_tile(1), per_tile(0), ALU.subtract).then_inc(exp_ready, 1)
            dve.wait_ge(exp_ready, 2)
            link(v.tensor_scalar(per_tile(2), per_tile(3), 1.0, None, ALU.add))
            link(v.reciprocal(per_tile(0), per_tile(2)))
            link(v.tensor_tensor(per_tile(1), per_tile(0), per_tile(3), ALU.mult))
            link(v.tensor_tensor(te(1), te(1), wide(per_tile(0)), ALU.mult))
            link(v.tensor_tensor(te(3), te(3), wide(per_tile(1)), ALU.mult))
            v.tensor_tensor(CW[:, :], route[:, TE:2 * TE], route[:, 3 * TE:4 * TE], ALU.add).then_inc(cw_ready, 1)
            dve.wait_ge(cw_ready, 1)

            def add_expert(k, s, e):
                need(dve, moe_ready, k + 1)
                for n in range(TOK // P):
                    t = s * (TOK // P) + n
                    w = CW[:, bass.ds(t * EXPERTS + e, 1)]
                    last = v.scalar_tensor_tensor(out=cols(H2, t), in0=bank[3][:, n * P:(n + 1) * P], scalar=w,
                                                  in1=cols(H2, t), op0=ALU.mult, op1=ALU.add)
                last.then_inc(moe_added, 1)

            STEPS = TILES * P // TOK
            with dve.Fori(0, EXPERTS) as e:
                with dve.Fori(0, STEPS) as s:
                    add_expert(e * STEPS + s, s, e)

            dve.wait_ge(moe_added, EXPERTS * STEPS)
            with dve.Fori(0, TILES) as t:
                v.bn_stats(cols(fstat, t, 6), cols(H2, t)).then_inc(fstat_ready, 1)
            dve.wait_ge(fstat_ready, TILES)
            moments(fstat[:, :], mean1[:, :], var[:, :], half[:, :], EPS_FFN)
            dve.wait_ge(rstd_ready, BATCHES + 3)

            def finish(t, p):
                b = t // TPB
                need(dve, stored[p], (t - p) * 8)
                v.tensor_scalar(fin[p][:, :], cols(H2, t), cols(mean1, t, 1), cols(rstd1, t, 1), ALU.subtract,
                                ALU.mult).then_inc(fin_a, 1)
                need(dve, fin_a, t + 1)
                v.tensor_tensor(fin[p][:, :], fin[p][:, :], cols(LNW, b), ALU.mult).then_inc(fin_b, 1)
                need(dve, fin_b, t + 1)
                v.tensor_tensor(fin[p][:, :], fin[p][:, :], cols(LNB, b), ALU.add).then_inc(fin_c, 1)
                need(dve, fin_c, t + 1)
                v.tensor_tensor(fin[p][:, :], fin[p][:, :], cols(X, t), ALU.add).then_inc(fin_ready, 1)

            tile_loop(dve, finish)


def kernel(**inputs):
    import concourse.bacc as _bacc
    from concourse.bass_utils import run_bass_kernel_spmd as _run

    def arr(name):
        return np.ascontiguousarray(inputs[name])

    def rows(name):
        return np.tile(arr(name)[None, :], (P, 1))

    parts = {
        "wqT": arr("L0_attn_W_q").T, "wkT": arr("L0_attn_W_k").T, "wvT": arr("L0_attn_W_v").T,
        "wkT2": arr("L0_attn_W_k").T, "woT": arr("L0_attn_W_o").T, "wmod": arr("L0_wmod"), "cT": arr("L0_c").T,
        "gn_w": arr("L0_attn_gn_weight")[:, None], "gn_b": arr("L0_attn_gn_bias")[:, None],
        "rwT": arr("L0_ffn_router_w").T, "r_b": rows("L0_ffn_router_b"),
        "ln_w": rows("L0_ffn_ln_w"), "ln_b": rows("L0_ffn_ln_b"),
    }
    w1, w2, b1 = arr("L0_ffn_w1"), arr("L0_ffn_w2"), arr("L0_ffn_b1")
    experts = np.concatenate([
        w1.transpose(0, 2, 1),
        w2.transpose(0, 2, 1).reshape(EXPERTS, FC, P, P).transpose(0, 2, 1, 3).reshape(EXPERTS, P, FC * P),
        b1.reshape(EXPERTS, FC, P).transpose(0, 2, 1)], axis=2)
    arrays = {
        "x": arr("L0_attn_x"),
        "weights": np.concatenate([parts[n] for n, _ in WEIGHTS], axis=1),
        "consts": np.concatenate(list(shape_constants().values()), axis=1),
        "experts": experts,
        "b2": arr("L0_ffn_b2"),
    }
    arrays = {k: np.ascontiguousarray(a) for k, a in arrays.items()}
    nc = _bacc.Bacc("TRN2", target_bir_lowering=False, num_devices=1)
    args = [nc.dram_tensor(k, a.shape, mybir.dt.from_np(a.dtype), kind="ExternalInput").ap() for k, a in arrays.items()]
    args.append(nc.dram_tensor("out", arrays["x"].shape, F32, kind="ExternalOutput").ap())
    build(nc, *args)
    return _run(nc, [arrays], core_ids=[0]).results[0]["out"]
```

```python
from contextlib import ExitStack

import numpy as np

import concourse.bass as bass
from concourse import mybir

F32 = mybir.dt.float32
I32 = mybir.dt.int32
ACT = mybir.ActivationFunctionType
ALU = mybir.AluOpType
AX = mybir.AxisListType

P = 128
HEADS = 16
DH = P // HEADS
BATCHES = 4
SEQ = 1024
TILES = BATCHES * SEQ // P
TPB = SEQ // P
GROUPS = 4
HPG = HEADS // GROUPS
LANE = 32 + DH
EXPERTS = 8
FF = 512
FC = FF // P
TOKENS = TILES * P
TOP_K = 2
SLOTS = 256
NS = SLOTS // P
REGION = TOKENS + SLOTS
NOWHERE = 8 * TOKENS
ROW = P + 1
WIDE = 4
RING = 4
STEPS = -(-(TOP_K * TOKENS // SLOTS + EXPERTS - 1) // RING) * RING
EPS = 1e-5
EPS_FFN = 1e-12


def shape_constants():
    gamma = 1.0 - 2.0 ** (-5.0 - np.arange(HEADS, dtype=np.float64))
    head = np.arange(P) // DH
    j, i = np.arange(P)[:, None], np.arange(P)[None, :]
    decay = np.where(i >= j, gamma[:, None, None] ** np.maximum(i - j, 0), 0.0) / np.sqrt(DH)
    decay = decay.transpose(1, 0, 2).reshape(P, HEADS * P)
    last = np.arange(TILES) % TPB == TPB - 1
    tables = {
        "ident": np.eye(P),
        "same_head": (head[:, None] == head[None, :]),
        "head_mean": (head[:, None] == head[None, :]) / DH,
        "decay": decay,
        "qdec": gamma[head][:, None] ** (i + 1) / np.sqrt(DH),
        "kdec": gamma[head][None, :] ** (P - 1 - j),
        "of_head": (head[:, None] == np.arange(HEADS)[None, :]),
        "carry": np.where(last[None, :], 0.0, gamma[head][:, None] ** P),
        "keep": np.tile(1.0 - last[None, :], (P, 1)),
        "before": (np.arange(P)[:, None] < np.arange(P)[None, :]),
        "ones": np.ones((P, P)),
        "region": np.tile(REGION * np.arange(EXPERTS)[None, :], (P, 1)),
        "token": np.arange(P)[:, None] + P * np.arange(TILES)[None, :],
        "rank": np.tile(np.arange(EXPERTS, 0, -1.0)[None, :], (P, 1)),
    }
    return {k: np.ascontiguousarray(v, np.float32) for k, v in tables.items()}


def plan_tables():
    e = np.arange(EXPERTS)
    tables = {
        "fill": np.tile(SLOTS * np.arange(TOKENS // SLOTS), EXPERTS),
        "upto": (e[None, :] <= e[:, None]).ravel(),
        "step": np.repeat(np.arange(STEPS), EXPERTS),
        "index": np.arange(STEPS),
        "start": REGION * e,
    }
    return {k: np.ascontiguousarray(v, np.float32) for k, v in tables.items()}


WEIGHTS = [("wqT", P), ("wkT", P), ("wvT", P), ("wkT2", P), ("woT", P), ("wmod", 6 * P), ("cT", BATCHES),
           ("gn_w", 1), ("gn_b", 1), ("rwT", EXPERTS), ("r_b", EXPERTS), ("ln_w", P), ("ln_b", P)]
EXPERT_COLS = FF + FC * P + FC + P


def offsets(widths):
    at, out = 0, {}
    for name, n in widths:
        out[name] = (at, at + n)
        at += n
    return out, at


def build(nc, x, weights, consts, experts, plan, out):
    const_at, const_cols = offsets([(k, v.shape[1]) for k, v in shape_constants().items()])
    weight_at, weight_cols = offsets(WEIGHTS)
    plan_at, plan_cols = offsets([(k, len(v)) for k, v in plan_tables().items()])
    dispatch = nc.dram_tensor("dispatch", (EXPERTS * REGION + SLOTS, ROW), F32).ap()
    returned = nc.dram_tensor("returned", (TOP_K * TOKENS, P), F32).ap()

    with ExitStack() as ctx:
        def sb(name, cols, parts=P, dtype=F32):
            return ctx.enter_context(nc.sbuf_tensor(name, [parts, cols], dtype))

        def sem(name):
            return ctx.enter_context(nc.semaphore(name))

        CONST = sb("CONST", const_cols)
        WGT = sb("WGT", weight_cols)

        def const(name):
            return CONST[:, const_at[name][0]:const_at[name][1]]

        def wgt(name):
            return WGT[:, weight_at[name][0]:weight_at[name][1]]

        X = sb("X", TILES * P)
        YT = sb("YT", TILES * P)
        ROWS = [sb(f"ROWS_{k}", TILES * ROW) for k in range(TOP_K)]
        CHOICE = sb("CHOICE", TOP_K * TILES)
        stat = sb("stat", TILES * 6)
        ystat = sb("ystat", TILES * 6)
        xstat = sb("xstat", TILES * 6)
        mean1, rstd1 = sb("mean1", TILES), sb("rstd1", TILES)
        mean2, rstd2 = sb("mean2", TILES), sb("rstd2", TILES)
        var = sb("var", TILES)
        half = sb("half", TILES)
        minus_half = sb("minus_half", TILES)
        silu = sb("silu", 3 * BATCHES)
        silu_bc = sb("silu_bc", BATCHES * P)
        shiftT, scaleT = sb("shiftT", TILES), sb("scaleT", TILES)
        MOD = sb("MOD", BATCHES * 4 * P)
        gate = sb("gate", 2 * BATCHES * P)
        WOG = sb("WOG", BATCHES * P)
        LNW, LNB = sb("LNW", BATCHES * P), sb("LNB", BATCHES * P)
        gn = sb("gn", 2 * BATCHES)
        gsc = sb("gsc", 4 * BATCHES)
        ga_t, gb_t = sb("gn_scale", TILES), sb("gn_shift", TILES)

        h0 = [sb(f"h0_{p}", P) for p in range(2)]
        hT = [sb(f"hT_{p}", P) for p in range(2)]
        QK = [sb(f"QK_{p}", 2 * P) for p in range(2)]
        Qm = [sb(f"Qm_{p}", HEADS * P) for p in range(2)]
        Qd = [sb(f"Qd_{p}", P) for p in range(2)]
        V = [sb(f"V_{p}", GROUPS * HPG * LANE) for p in range(2)]
        Kd = [sb(f"Kd_{p}", P) for p in range(2)]
        PR = [sb(f"PR_{p}", HEADS * P) for p in range(2)]
        UM = sb("UM", P)
        STATE = [sb(f"STATE_{p}", P) for p in range(2)]
        yn = [sb(f"yn_{g}", WIDE * P) for g in range(2)]
        hn = [sb(f"hn_{g}", WIDE * P) for g in range(2)]
        h2 = [sb(f"h2_{g}", WIDE * P) for g in range(2)]
        h2t = [sb(f"h2t_{g}", WIDE * P) for g in range(2)]
        BE = TPB * EXPERTS
        route = sb("route", 4 * BE)
        CHOSEN = sb("CHOSEN", BE)
        CHOSEN_BEFORE = sb("CHOSEN_BEFORE", BE + EXPERTS)
        topv = sb("topv", 4 * TPB)
        slotf = sb("slotf", TOP_K * TPB)
        SLOT = sb("SLOT", TOP_K * TILES, dtype=I32)
        PLAN = sb("PLAN", plan_cols, 1)
        plan_w = sb("plan_w", 4 * EXPERTS + 2 * STEPS * EXPERTS + 4 * STEPS + EXPERTS * (TOKENS // SLOTS), 1)
        STEP_START = sb("STEP_START", STEPS, 1, I32)
        STEP_EXPERT = sb("STEP_EXPERT", STEPS, 1, I32)
        FILLED = sb("FILLED", EXPERTS, 1, I32)
        PADDING = sb("PADDING", NS * ROW)
        IN = [sb(f"IN_{r}", NS * ROW) for r in range(RING)]
        EW = [sb(f"EW_{r}", EXPERT_COLS) for r in range(RING)]
        DEST = [sb(f"DEST_{p}", NS, dtype=I32) for p in range(2)]
        INT = [sb(f"INT_{p}", SLOTS) for p in range(2)]
        HID = [sb(f"HID_{f}", SLOTS) for f in range(FC)]
        RES = [sb(f"RES_{p}", SLOTS) for p in range(2)]
        tick = sb("tick", 2)
        BACK = [PR[p][:, 0:TOP_K * WIDE * P] for p in range(2)]
        fin = [Qm[p][:, 0:WIDE * P] for p in range(2)]
        fstat = sb("fstat", TILES * 6)

        bank = [ctx.enter_context(nc.psum_tensor(f"bank{n}", [P, 512], F32)) for n in range(8)]
        TB, QB, KB, YB = bank[0], bank[1], bank[2], bank[3]
        SC = bank[4:8]

        x_loaded = [sem(f"x_loaded{b}") for b in range(BATCHES)]
        const_loaded, wgt_loaded = sem("const_loaded"), sem("wgt_loaded")
        dve_chain, act_step, pool_step, silu_ready = sem("dve_chain"), sem("act_step"), sem("pool_step"), sem("silu_ready")
        stat_ready, tick_done = sem("stat_ready"), sem("tick_done")
        var_ready, rstd_ready = sem("var_ready"), sem("rstd_ready")
        mod_ready, mod_read = sem("mod_ready"), sem("mod_read")
        h0_ready, h0T_ready, hT_ready = sem("h0_ready"), sem("h0T_ready"), sem("hT_ready")
        qk_ps, qk_ready, kv_ready, qm_ready = sem("qk_ps"), sem("qk_ready"), sem("kv_ready"), sem("qm_ready")
        kvs_ready, qd_ready = sem("kvs_ready"), sem("qd_ready")
        sc_ready, p_ready = sem("sc_ready"), sem("p_ready")
        u_ready, um_ready, s_ready = sem("u_ready"), sem("um_ready"), sem("s_ready")
        y_ready, YT_ready = sem("y_ready"), sem("YT_ready")
        ystat_ready = sem("ystat_ready")
        gmean_ready, gn_ready = sem("gmean_ready"), sem("gn_ready")
        yn_ready, att_ready, x2_ready = sem("yn_ready"), sem("att_ready"), sem("x2_ready")
        n2_ready, m2_ready, h2_ready = sem("n2_ready"), sem("m2_ready"), sem("h2_ready")
        h2T_ready, h2t_ready, lg_ready, lg_read = sem("h2T_ready"), sem("h2t_ready"), sem("lg_ready"), sem("lg_read")
        row_ready, exp_in, exp_out = sem("row_ready"), sem("exp_in"), sem("exp_out")
        chosen_ready, rank_ready, rank_read = sem("chosen_ready"), sem("rank_ready"), sem("rank_read")
        slot_ready, scattered, padded = sem("slot_ready"), sem("scattered"), sem("padded")
        plan_loaded, count_ready, plan_ready = sem("plan_loaded"), sem("count_ready"), sem("plan_ready")
        in_loaded = [sem(f"in_loaded{r}") for r in range(RING)]
        ew_loaded = [sem(f"ew_loaded{r}") for r in range(RING)]
        inT_ps, inT_ready, dest_ready = sem("inT_ps"), sem("inT_ready"), sem("dest_ready")
        hid_ps, hid_ready, moe_ready, res_ready = sem("hid_ps"), sem("hid_ready"), sem("moe_ready"), sem("res_ready")
        sent_back = [sem(f"sent_back{p}") for p in range(2)]
        back_loaded = [sem(f"back_loaded{p}") for p in range(2)]
        sum_a, sum_b, fstat_ready = sem("sum_a"), sem("sum_b"), sem("fstat_ready")
        last_ready = sem("last_ready")
        fin_a, fin_b, fin_ready = sem("fin_a"), sem("fin_b"), sem("fin_ready")
        stored = [sem(f"stored{p}") for p in range(2)]

        block = ctx.enter_context(nc.Block())

        def need(eng, s, value):
            if isinstance(value, int) and value <= 0:
                return
            eng.wait_ge(s, value)

        def tile_loop(eng, step):
            step(0, 0)
            step(1, 1)
            with eng.Fori(1, TILES // 2 - 1) as pair:
                step(2 * pair, 0)
                step(2 * pair + 1, 1)
            step(TILES - 2, 0)
            step(TILES - 1, 1)

        def group_loop(eng, step):
            step(0, 0)
            step(1, 1)
            with eng.Fori(1, TILES // WIDE // 2 - 1) as pair:
                step(2 * pair, 0)
                step(2 * pair + 1, 1)
            step(TILES // WIDE - 2, 0)
            step(TILES // WIDE - 1, 1)

        def expert_loop(eng, step):
            for r in range(RING):
                step(r, r)
            with eng.Fori(1, STEPS // RING - 1) as turn:
                for r in range(RING):
                    step(RING * turn + r, r)
            for r in range(RING):
                step(STEPS - RING + r, r)

        def cols(tensor, t, n=P):
            return tensor[:, t * n:(t + 1) * n] if isinstance(t, int) else tensor[:, bass.ds(t * n, n)]

        def last_tile(t):
            return isinstance(t, int) and t == TILES - 1

        def near_end(t):
            return isinstance(t, int) and t >= TILES - 2

        @block.sync
        def _(sp):
            x_v = x.rearrange("b (n p) d -> p b n d", p=P)
            for b in range(BATCHES):
                sp.dma_start(X[:, b * SEQ:(b + 1) * SEQ].rearrange("p (n d) -> p n d", d=P), x_v[:, b])\
                  .then_inc(x_loaded[b], 16)
                if b == 0:
                    sp.dma_start(WGT[:, :], weights).then_inc(wgt_loaded, 16)
                    sp.dma_start(CONST[:, :], consts).then_inc(const_loaded, 16)

            sp.dma_start(PLAN[:, :], plan).then_inc(plan_loaded, 16)

            sp.wait_ge(plan_ready, 3)
            for e in range(EXPERTS):
                end = sp.value_load(FILLED[0:1, e:e + 1], min_val=e * REGION, max_val=e * REGION + TOKENS)
                sp.dma_start(dispatch[bass.ds(end, SLOTS), :].rearrange("(n p) d -> p n d", p=P),
                             PADDING[:, :].rearrange("p (n d) -> p n d", d=ROW)).then_inc(padded, 16)
            sp.dma_start(dispatch[EXPERTS * REGION:, :].rearrange("(n p) d -> p n d", p=P),
                         PADDING[:, :].rearrange("p (n d) -> p n d", d=ROW)).then_inc(padded, 16)
            sp.wait_ge(padded, 16 * (EXPERTS + 1))

            def load_weights(i, r):
                need(sp, res_ready, i - RING + 1)
                e = sp.value_load(cols(STEP_EXPERT, i, 1), min_val=0, max_val=EXPERTS - 1)
                sp.dma_start(EW[r][:, :], experts[bass.ds(e, 1)].rearrange("a p n -> p (a n)")).then_inc(ew_loaded[r], 16)

            def load_rows(i, r):
                start = sp.value_load(cols(STEP_START, i, 1), min_val=0, max_val=EXPERTS * REGION)
                sp.dma_start(IN[r][:, :].rearrange("p (n d) -> p n d", d=ROW),
                             dispatch[bass.ds(start, SLOTS), :].rearrange("(n p) d -> p n d", p=P))\
                  .then_inc(in_loaded[r], 16)

            def load_step(i, r):
                if not (isinstance(i, int) and i < RING):
                    load_weights(i, r)
                load_rows(i, r)

            for r in range(RING):
                load_weights(r, r)
            sp.wait_ge(scattered, 16 * TOP_K * TILES)
            expert_loop(sp, load_step)

            for p in range(2):
                sp.wait_ge(sent_back[p], 16 * NS * STEPS // 2)
            back_v = returned.rearrange("(k g n p) d -> g p k n d", k=TOP_K, n=WIDE, p=P)
            out_v = out.rearrange("b (g n p) d -> (b g) p n d", n=WIDE, p=P)

            def at_group(view, g):
                return view[g] if isinstance(g, int) else view[bass.ds(g, 1)]

            def load_back(g, p):
                need(sp, sum_b, WIDE * (g - 1))
                dst = BACK[p][:, :].rearrange("p (k n d) -> p k n d", k=TOP_K, d=P)
                for k in range(TOP_K):
                    src = back_v[g][:, k] if isinstance(g, int) else \
                        back_v[bass.ds(g, 1), :, k].rearrange("g p n d -> p (g n) d")
                    sp.dma_start(dst[:, k], src).then_inc(back_loaded[p], 16)

            def store(g, p):
                need(sp, fin_ready, g + 1)
                dst = out_v[g] if isinstance(g, int) else out_v[bass.ds(g, 1)].rearrange("g p n d -> p (g n) d")
                sp.dma_start(dst, fin[p][:, :].rearrange("p (n d) -> p n d", d=P)).then_inc(stored[p], 16)

            group_loop(sp, load_back)
            group_loop(sp, store)
            for p in range(2):
                sp.wait_ge(stored[p], 16 * TILES // WIDE // 2)

        @block.gpsimd
        def _(pool):
            nc.gpsimd.memset(minus_half[:, :], -0.5).then_inc(pool_step, 1)
            nc.gpsimd.memset(STATE[0][:, :], 0.0).then_inc(pool_step, 1)
            nc.gpsimd.memset(CHOSEN_BEFORE[:, :], 0.0).then_inc(pool_step, 1)
            nc.gpsimd.memset(tick[:, :], 0.0).then_inc(pool_step, 1)
            nc.gpsimd.memset(PADDING[:, :], 0.0).then_inc(pool_step, 1)
            pool.wait_ge(pool_step, 5)
            for p in range(2):
                nc.gpsimd.memset(V[p][:, :], 0.0).then_inc(pool_step, 1)
            pad = PADDING[:, :].rearrange("p (n d) -> p n d", d=ROW)
            nc.gpsimd.memset(pad[:, :, P:ROW], float(NOWHERE)).then_inc(pool_step, 1)
            step = [0]

            def rsqrt(dst, src):
                step[0] += 1
                pool.wait_ge(var_ready, step[0])
                n = dst.shape[1]
                nc.gpsimd.tensor_tensor(dst, src, minus_half[:, 0:n], ALU.pow).then_inc(rstd_ready, 1)

            for b in range(BATCHES):
                rsqrt(rstd1[:, b * TPB:(b + 1) * TPB], var[:, b * TPB:(b + 1) * TPB])
            def queries(u, p):
                need(pool, qk_ready, u + 1)
                need(pool, sc_ready, GROUPS * (u - 1))
                nc.gpsimd.tensor_tensor(Qm[p][:, :].rearrange("p (h i) -> p h i", i=P),
                                        QK[p][:, 0:P].unsqueeze(1).broadcast_to((P, HEADS, P)),
                                        const("of_head").unsqueeze(2).broadcast_to((P, HEADS, P)),
                                        ALU.mult).then_inc(qm_ready, 1)
                need(pool, y_ready, u - 1)
                nc.gpsimd.tensor_tensor(Qd[p][:, :], QK[p][:, 0:P], const("qdec"), ALU.mult).then_inc(qd_ready, 1)

            def a_step(t, p):
                if not last_tile(t):
                    queries(t + 1, 1 - p)

            pool.wait_ge(const_loaded, 16)
            queries(0, 0)
            tile_loop(pool, a_step)

            rsqrt(gsc[:, 0:BATCHES], gsc[:, BATCHES:2 * BATCHES])
            for b in range(BATCHES):
                at = slice(b * TPB, (b + 1) * TPB)
                rsqrt(rstd2[:, at], var[:, at])

            for b in range(BATCHES):
                pool.wait_ge(slot_ready, b + 1)
                pool.wait_ge(row_ready, 2 * TOP_K * (b + 1))
                for n in range(TPB):
                    t = b * TPB + n
                    for k in range(TOP_K):
                        at = (b * TOP_K + k) * TPB + n
                        nc.gpsimd.indirect_dma_start(
                            dispatch, bass.IndirectOffsetOnAxis(SLOT[:, at:at + 1], 0),
                            ROWS[k][:, t * ROW:(t + 1) * ROW], None).then_inc(scattered, 16)

            def send_back(i, r):
                p = r % 2
                need(pool, tick_done, i)
                need(pool, res_ready, i + 1)
                nc.gpsimd.tensor_tensor(tick[:, 0:1], tick[:, 1:2], tick[:, 1:2], ALU.add).then_inc(tick_done, 1)
                for n in range(NS):
                    nc.gpsimd.indirect_dma_start(
                        returned, bass.IndirectOffsetOnAxis(DEST[p][:, n:n + 1], 0),
                        RES[p][:, n * P:(n + 1) * P], None,
                        bounds_check=TOP_K * TOKENS - 1, oob_is_err=False).then_inc(sent_back[p], 16)

            expert_loop(pool, send_back)
            rsqrt(rstd1[:, :], var[:, :])

        @block.scalar
        def _(act):
            act.wait_ge(wgt_loaded, 16)
            nc.scalar.activation(silu[:, 0:BATCHES], wgt("cT"), ACT.Exp, scale=-1.0).then_inc(act_step, 1)

            def front(u, p):
                need(act, h0T_ready, u + 1)
                need(act, kv_ready, u - 1)
                nc.scalar.activation(hT[p][:, :], TB[:, 0:P], ACT.Identity, bias=cols(shiftT, u, 1),
                                     scale=cols(scaleT, u, 1)).then_inc(hT_ready, 1)

            def queries_keys(u, p):
                need(act, qk_ps, u + 1)
                need(act, sc_ready, GROUPS * (u - 1))
                need(act, qd_ready, u - 1)
                nc.scalar.activation(QK[p][:, :], QB[:, 0:2 * P], ACT.Copy).then_inc(qk_ready, 1)

            def y_back(t):
                need(act, y_ready, t + 1)
                nc.scalar.activation(cols(YT, t), YB[:, 0:P], ACT.Copy).then_inc(YT_ready, 1)

            def step(t, p):
                if not last_tile(t):
                    queries_keys(t + 1, 1 - p)
                if not near_end(t):
                    front(t + 2, p)
                y_back(t)

            act.wait_ge(const_loaded, 16)
            act.wait_ge(mod_read, 2)
            front(0, 0)
            front(1, 1)
            queries_keys(0, 0)
            tile_loop(act, step)

            act.wait_ge(gn_ready, 1)
            act.wait_ge(YT_ready, TILES)

            def norm_y(g, p):
                need(act, att_ready, g - 1)
                for n in range(WIDE):
                    t = g * WIDE + n
                    last = nc.scalar.activation(yn[p][:, n * P:(n + 1) * P], cols(YT, t), ACT.Identity,
                                                bias=cols(gb_t, t, 1), scale=cols(ga_t, t, 1))
                last.then_inc(yn_ready, 1)

            group_loop(act, norm_y)

            for b in range(BATCHES):
                for p in range(2):
                    g = 2 * b + p
                    act.wait_ge(h2T_ready, g + 1)
                    need(act, lg_ready, g - 1)
                    nc.scalar.activation(h2t[p][:, :], bank[2 + p][:, :], ACT.Copy).then_inc(h2t_ready, 1)
                    for k in range(TOP_K):
                        dst = ROWS[k][:, g * WIDE * ROW:(g + 1) * WIDE * ROW].rearrange("p (n d) -> p n d", d=ROW)
                        nc.scalar.activation(dst[:, :, 0:P], h2[p][:, :].rearrange("p (n d) -> p n d", d=P), ACT.Copy)\
                            .then_inc(row_ready, 1)
                act.wait_ge(exp_in, b + 1)
                nc.scalar.activation(topv[:, 3 * TPB:4 * TPB], topv[:, 2 * TPB:3 * TPB], ACT.Exp).then_inc(exp_out, 1)

            def gelu(i, r):
                for f in range(FC):
                    need(act, hid_ps, i * FC + f + 1)
                    if f == 0:
                        need(act, moe_ready, i)
                    nc.scalar.activation(HID[f][:, :], bank[f][:, 0:SLOTS], ACT.Gelu,
                                         bias=EW[r][:, FF + FC * P + f:FF + FC * P + f + 1]).then_inc(hid_ready, 1)

            expert_loop(act, gelu)

            act.wait_ge(last_ready, 1)

            def normalise_sum(g, p):
                need(act, fin_ready, g - 1)
                need(act, stored[p], (g - p) * 8)
                for n in range(WIDE):
                    t = g * WIDE + n
                    at = t * ROW
                    src = ROWS[0][:, at:at + P] if isinstance(t, int) else ROWS[0][:, bass.ds(at, P)]
                    last = nc.scalar.activation(fin[p][:, n * P:(n + 1) * P], src, ACT.Identity,
                                                bias=cols(mean1, t, 1), scale=cols(rstd1, t, 1))
                last.then_inc(fin_a, 1)

            group_loop(act, normalise_sum)

        @block.tensor
        def _(pe):
            mm = nc.tensor.matmul
            pe.wait_ge(wgt_loaded, 16)
            pe.wait_ge(silu_ready, 1)
            for n in range(2):
                mm(bank[4][:, n * BATCHES:(n + 1) * BATCHES], wgt("wmod")[:, n * P:(n + 1) * P],
                   silu[:, 2 * BATCHES:3 * BATCHES], start=True, stop=True, skip_group_check=True)\
                    .then_inc(mod_ready, 1)
            for b in range(BATCHES):
                mm(bank[b][:, :], cols(silu_bc, b), wgt("wmod")[:, 2 * P:6 * P],
                   start=True, stop=True).then_inc(mod_ready, 1)

            def transpose_in(u, p):
                need(pe, h0_ready, u + 1)
                need(pe, hT_ready, u)
                nc.tensor.transpose(TB[:, 0:P], h0[p][:, :], const("ident")).then_inc(h0T_ready, 1)

            def project(u, p):
                need(pe, hT_ready, u + 1)
                need(pe, qk_ready, u)
                mm(QB[:, 0:P], wgt("wqT"), hT[p][:, :], start=True, stop=True)
                mm(QB[:, P:2 * P], wgt("wkT"), hT[p][:, :], start=True, stop=True, skip_group_check=True)\
                    .then_inc(qk_ps, 1)
                need(pe, kvs_ready, u)
                need(pe, um_ready, u - 1)
                mm(KB[:, 0:2 * P], hT[p][:, :], WGT[:, weight_at["wvT"][0]:weight_at["wkT2"][1]],
                   start=True, stop=True, skip_group_check=True).then_inc(kv_ready, 1)

            def scores(t, p):
                need(pe, qm_ready, t + 1)
                for g in range(GROUPS):
                    need(pe, p_ready, GROUPS * (t - 1) + g + 1)
                    mm(SC[g][:, :], QK[p][:, P:2 * P], Qm[p][:, g * HPG * P:(g + 1) * HPG * P], start=True,
                       stop=True).then_inc(sc_ready, 1)

            def state_update(t, p):
                need(pe, kvs_ready, min(t + 2, TILES) if isinstance(t, int) else t + 2)
                need(pe, um_ready, t)
                values = V[p][:, :].rearrange("p (h c) -> p h c", c=LANE)[:, :, 0:DH]
                mm(KB[:, 2 * P:3 * P], Kd[p][:, :], values, start=True, stop=True, skip_group_check=True)\
                    .then_inc(u_ready, 1)

            def outputs(t, p):
                need(pe, YT_ready, t)
                need(pe, qd_ready, t + 1)
                need(pe, s_ready, t)
                mm(YB[:, 0:P], STATE[p][:, :], Qd[p][:, :], start=True, stop=False, skip_group_check=True)
                need(pe, p_ready, GROUPS * (t + 1))
                for a in range(HPG):
                    for g in range(GROUPS):
                        at, h = g * HPG * LANE + 32 * a, g * HPG + a
                        last = mm(YB[32 * g:32 * (g + 1), 0:P], V[p][:, at:at + 32], PR[p][:, h * P:(h + 1) * P],
                                  start=False, stop=(a == HPG - 1), skip_group_check=True)
                last.then_inc(y_ready, 1)

            def step(t, p):
                if not last_tile(t):
                    project(t + 1, 1 - p)
                scores(t, p)
                if not near_end(t):
                    transpose_in(t + 2, p)
                state_update(t, p)
                outputs(t, p)

            pe.wait_ge(const_loaded, 16)
            pe.wait_ge(mod_read, 2 + BATCHES)
            transpose_in(0, 0)
            transpose_in(1, 1)
            project(0, 0)
            pe.wait_ge(pool_step, 8)
            tile_loop(pe, step)

            pe.wait_ge(gmean_ready, 1)
            mm(bank[4][:, 0:2 * BATCHES], const("head_mean"), gn[:, :], start=True, stop=True).then_inc(gmean_ready, 1)

            def attend(g, p):
                need(pe, yn_ready, g + 1)
                need(pe, x2_ready, g - 1)
                b = g // 2
                for n in range(WIDE):
                    last = mm(bank[p][:, n * P:(n + 1) * P], yn[p][:, n * P:(n + 1) * P], cols(WOG, b), start=True,
                              stop=True, skip_group_check=True)
                last.then_inc(att_ready, 1)

            for g in range(2 * BATCHES):
                attend(g, g % 2)

            for b in range(BATCHES):
                for p in range(2):
                    g = 2 * b + p
                    pe.wait_ge(h2_ready, g + 1)
                    need(pe, h2t_ready, g - 1)
                    for n in range(WIDE):
                        at = slice(n * P, (n + 1) * P)
                        last = nc.tensor.transpose(bank[2 + p][:, at], h2[p][:, at], const("ident"))
                    last.then_inc(h2T_ready, 1)
                for p in range(2):
                    g = 2 * b + p
                    pe.wait_ge(h2t_ready, g + 1)
                    need(pe, lg_read, b)
                    for n in range(WIDE):
                        at = (p * WIDE + n) * EXPERTS
                        last = mm(bank[4][:, at:at + EXPERTS], h2t[p][:, n * P:(n + 1) * P], wgt("rwT"), start=True,
                                  stop=True, skip_group_check=True)
                    last.then_inc(lg_ready, 1)
                pe.wait_ge(chosen_ready, b + 1)
                need(pe, rank_read, b)
                mm(bank[5][:, 0:BE], const("before"), CHOSEN[:, :], start=True, stop=False)
                mm(bank[5][:, 0:BE], const("ones"), CHOSEN_BEFORE[:, 0:BE], start=False, stop=True)\
                    .then_inc(rank_ready, 1)
            mm(bank[6][:, 0:EXPERTS], const("ones"), CHOSEN_BEFORE[:, BE:], start=True, stop=True)\
                .then_inc(count_ready, 1)

            pe.wait_ge(plan_ready, 3)

            def transpose_rows(r):
                for n in range(NS):
                    last = nc.tensor.transpose(bank[4 + r % 2][:, n * P:(n + 1) * P], IN[r][:, n * ROW:n * ROW + P],
                                               const("ident"))
                last.then_inc(inT_ps, 1)

            def expert_step(i, r):
                p = r % 2
                for f in range(FC):
                    if f == 0:
                        need(pe, inT_ready, i + 1)
                    need(pe, hid_ready, (i - 1) * FC + f + 1)
                    mm(bank[f][:, 0:SLOTS], EW[r][:, f * P:(f + 1) * P], INT[p][:, :], start=True, stop=True)\
                        .then_inc(hid_ps, 1)

            def second_layer(i, r):
                p = r % 2
                need(pe, res_ready, i - 1)
                for n in range(NS):
                    for f in range(FC):
                        if n == 0:
                            need(pe, hid_ready, i * FC + f + 1)
                        last = mm(bank[6 + p][:, n * P:(n + 1) * P], HID[f][:, n * P:(n + 1) * P],
                                  EW[r][:, FF + f * P:FF + (f + 1) * P], start=(f == 0), stop=(f == FC - 1),
                                  skip_group_check=True)
                last.then_inc(moe_ready, 1)

            def loaded(s, r, turn):
                pe.wait_ge(s[r], 16 * (turn + 1))

            def ring_round(turn, last):
                for r in range(RING):
                    i = RING * turn + r
                    loaded(ew_loaded, r, turn)
                    expert_step(i, r)
                    if not (last and r == RING - 1):
                        rn = (r + 1) % RING
                        loaded(in_loaded, rn, turn + (r == RING - 1))
                        transpose_rows(rn)
                    second_layer(i, r)

            loaded(in_loaded, 0, 0)
            transpose_rows(0)
            ring_round(0, False)
            with pe.Fori(1, STEPS // RING - 1) as turn:
                ring_round(turn, False)
            ring_round(STEPS // RING - 1, True)

        @block.vector
        def _(dve):
            v = nc.vector
            chain = [0]

            def link(ins):
                chain[0] += 1
                ins.then_inc(dve_chain, 1)
                dve.wait_ge(dve_chain, chain[0])

            def moments(stats, mean, variance, tmp, eps):
                s = stats.rearrange("p (t s) -> p t s", s=6)
                link(v.tensor_tensor(tmp, s[:, :, 1], s[:, :, 4], ALU.subtract))
                link(v.tensor_tensor(mean, s[:, :, 1], s[:, :, 4], ALU.add))
                link(v.tensor_scalar(mean, mean, 0.5, None, ALU.mult))
                link(v.tensor_tensor(tmp, tmp, tmp, ALU.mult))
                link(v.tensor_tensor(variance, s[:, :, 2], s[:, :, 5], ALU.add))
                link(v.tensor_scalar(variance, variance, 1.0 / P, eps, ALU.mult, ALU.add))
                v.scalar_tensor_tensor(out=variance, in0=tmp, scalar=0.25, in1=variance, op0=ALU.mult,
                                       op1=ALU.add).then_inc(var_ready, 1)

            def per_batch(ap):
                return ap.unsqueeze(2).broadcast_to((P, BATCHES, TPB))

            dve.wait_ge(act_step, 1)
            link(v.tensor_scalar(silu[:, 0:BATCHES], silu[:, 0:BATCHES], 1.0, None, ALU.add))
            link(v.reciprocal(silu[:, BATCHES:2 * BATCHES], silu[:, 0:BATCHES]))
            link(v.tensor_tensor(silu[:, 2 * BATCHES:3 * BATCHES], silu[:, BATCHES:2 * BATCHES], wgt("cT"), ALU.mult))
            v.tensor_copy(silu_bc[:, :].rearrange("p (b m) -> p b m", b=BATCHES),
                          silu[:, 2 * BATCHES:3 * BATCHES].unsqueeze(2).broadcast_to((P, BATCHES, P)))\
             .then_inc(silu_ready, 1)

            for b in range(BATCHES):
                dve.wait_ge(x_loaded[b], 16)
                with dve.Fori(b * TPB, (b + 1) * TPB) as t:
                    v.bn_stats(cols(stat, t, 6), cols(X, t)).then_inc(stat_ready, 1)
                dve.wait_ge(stat_ready, (b + 1) * TPB)
                at = slice(b * TPB, (b + 1) * TPB)
                moments(stat[:, b * TPB * 6:(b + 1) * TPB * 6], mean1[:, at], var[:, at], half[:, at], EPS)

            dve.wait_ge(mod_ready, 2)
            sa, ca = bank[4][:, 0:BATCHES], bank[4][:, BATCHES:2 * BATCHES]
            v.tensor_copy(shiftT[:, :].rearrange("p (b t) -> p b t", b=BATCHES), per_batch(sa)).then_inc(mod_read, 1)
            v.tensor_scalar(scaleT[:, :].rearrange("p (b t) -> p b t", b=BATCHES), per_batch(ca), 1.0, None,
                            ALU.add).then_inc(mod_read, 1)
            for b in range(BATCHES):
                dve.wait_ge(mod_ready, 3 + b)
                v.tensor_copy(MOD[:, b * 4 * P:(b + 1) * 4 * P], bank[b][:, :]).then_inc(mod_read, 1)
            dve.wait_ge(mod_read, 2 + BATCHES)
            mod = MOD[:, :].rearrange("p (b k d) -> p b k d", b=BATCHES, k=4)
            three = lambda tensor: tensor[:, 0:BATCHES * P].rearrange("p (b d) -> p b d", b=BATCHES)
            spread = lambda ap: ap.unsqueeze(1).broadcast_to((P, BATCHES, P))

            def clamp_gate(k):
                g = mod[:, :, k, :]
                hi = gate[:, BATCHES * P:].rearrange("p (b d) -> p b d", b=BATCHES)
                link(v.scalar_tensor_tensor(out=hi, in0=g, scalar=-1.0, in1=g, op0=ALU.mult, op1=ALU.max))
                link(v.tensor_scalar(hi, hi, 0.25, None, ALU.max))
                link(v.tensor_scalar(three(gate), g, 0.0, 2.0, ALU.is_ge, ALU.mult))
                link(v.scalar_tensor_tensor(out=gate[:, 0:BATCHES * P], in0=gate[:, 0:BATCHES * P], scalar=-1.0,
                                            in1=gate[:, BATCHES * P:], op0=ALU.add, op1=ALU.mult))

            clamp_gate(0)
            link(v.tensor_tensor(three(WOG), three(gate), spread(wgt("woT")), ALU.mult))
            clamp_gate(3)
            link(v.tensor_tensor(three(LNW), three(gate), spread(wgt("ln_w")), ALU.mult))
            link(v.tensor_tensor(three(LNB), three(gate), spread(wgt("ln_b")), ALU.mult))
            link(v.tensor_scalar(mod[:, :, 2, :], mod[:, :, 2, :], 1.0, None, ALU.add))

            def normalise(u, p):
                need(dve, h0T_ready, u - 1)
                v.tensor_scalar(h0[p][:, :], cols(X, u), cols(mean1, u, 1), cols(rstd1, u, 1), ALU.subtract,
                                ALU.mult).then_inc(h0_ready, 1)

            def keys_values(u, p):
                need(dve, y_ready, u - 1)
                need(dve, kv_ready, u + 1)
                v.tensor_copy(V[p][:, :].rearrange("p (h c) -> p h c", c=LANE)[:, :, 0:DH],
                              KB[:, 0:P].rearrange("p (h d) -> p h d", d=DH))
                v.tensor_tensor(Kd[p][:, :], KB[:, P:2 * P], const("kdec"), ALU.mult).then_inc(kvs_ready, 1)

            def mask(t, p):
                for g in range(GROUPS):
                    need(dve, sc_ready, GROUPS * t + g + 1)
                    if g == 0:
                        need(dve, y_ready, t - 1)
                    at = slice(g * HPG * P, (g + 1) * HPG * P)
                    v.tensor_tensor(PR[p][:, at], SC[g][:, :], const("decay")[:, at], ALU.mult).then_inc(p_ready, 1)

            def state(t, p):
                need(dve, u_ready, t + 1)
                need(dve, s_ready, t)
                v.scalar_tensor_tensor(out=UM[:, :], in0=KB[:, 2 * P:3 * P], scalar=cols(const("keep"), t, 1),
                                       in1=const("same_head"), op0=ALU.mult, op1=ALU.mult).then_inc(um_ready, 1)
                need(dve, um_ready, t + 1)
                need(dve, y_ready, t)
                v.scalar_tensor_tensor(out=STATE[1 - p][:, :], in0=STATE[p][:, :], scalar=cols(const("carry"), t, 1),
                                       in1=UM[:, :], op0=ALU.mult, op1=ALU.add).then_inc(s_ready, 1)

            def y_stats(t):
                v.bn_stats(cols(ystat, t, 6), cols(YT, t)).then_inc(ystat_ready, 1)

            def step(t, p):
                if not last_tile(t):
                    keys_values(t + 1, 1 - p)
                if not near_end(t):
                    normalise(t + 2, p)
                need(dve, YT_ready, t)
                mask(t, p)
                if not (isinstance(t, int) and t == 0):
                    y_stats(t - 1)
                state(t, p)

            dve.wait_ge(rstd_ready, BATCHES)
            dve.wait_ge(pool_step, 8)
            normalise(0, 0)
            normalise(1, 1)
            keys_values(0, 0)
            tile_loop(dve, step)
            dve.wait_ge(YT_ready, TILES)
            y_stats(TILES - 1)

            dve.wait_ge(ystat_ready, TILES)
            ys = ystat[:, :].rearrange("p (b n s) -> p b n s", b=BATCHES, s=3)
            mu, m2 = ys[:, :, :, 1], ys[:, :, :, 2]
            mean_c, square_c = gn[:, 0:BATCHES], gn[:, BATCHES:]
            sq = stat[:, 0:2 * TILES].rearrange("p (b n) -> p b n", b=BATCHES)
            link(v.tensor_reduce(mean_c, mu, AX.X, ALU.add))
            link(v.tensor_scalar(mean_c, mean_c, 1.0 / (2 * TPB), None, ALU.mult))
            link(v.tensor_tensor(sq, mu, mu, ALU.mult))
            link(v.tensor_scalar(sq, sq, P / 2.0, None, ALU.mult))
            link(v.tensor_tensor(sq, sq, m2, ALU.add))
            link(v.tensor_reduce(square_c, sq, AX.X, ALU.add))
            v.tensor_scalar(square_c, square_c, 1.0 / SEQ, None, ALU.mult).then_inc(gmean_ready, 1)
            dve.wait_ge(gmean_ready, 2)
            mean_h, square_h = gsc[:, 2 * BATCHES:3 * BATCHES], gsc[:, 3 * BATCHES:]
            var_h, rstd_h = gsc[:, BATCHES:2 * BATCHES], gsc[:, 0:BATCHES]
            link(v.tensor_copy(gsc[:, 2 * BATCHES:], bank[4][:, 0:2 * BATCHES]))
            link(v.tensor_tensor(var_h, mean_h, mean_h, ALU.mult))
            link(v.tensor_tensor(var_h, square_h, var_h, ALU.subtract))
            v.tensor_scalar(var_h, var_h, EPS, None, ALU.add).then_inc(var_ready, 1)
            dve.wait_ge(rstd_ready, BATCHES + 1)
            link(v.tensor_scalar(rstd_h, rstd_h, wgt("gn_w"), None, ALU.mult))
            link(v.tensor_tensor(mean_h, mean_h, rstd_h, ALU.mult))
            link(v.tensor_scalar(mean_h, mean_h, -1.0, wgt("gn_b"), ALU.mult, ALU.add))
            link(v.tensor_copy(ga_t[:, :].rearrange("p (b t) -> p b t", b=BATCHES), per_batch(rstd_h)))
            v.tensor_copy(gb_t[:, :].rearrange("p (b t) -> p b t", b=BATCHES), per_batch(mean_h)).then_inc(gn_ready, 1)

            for b in range(BATCHES):
                for p in range(2):
                    g = 2 * b + p
                    dve.wait_ge(att_ready, g + 1)
                    x4 = X[:, g * WIDE * P:(g + 1) * WIDE * P]
                    v.tensor_tensor(x4, bank[p][:, :], x4, ALU.add).then_inc(x2_ready, 1)
                for p in range(2):
                    g = 2 * b + p
                    dve.wait_ge(x2_ready, g + 1)
                    for n in range(WIDE):
                        t = g * WIDE + n
                        last = v.bn_stats(cols(xstat, t, 6), cols(X, t))
                link(last)
                at = slice(b * TPB, (b + 1) * TPB)
                moments(xstat[:, b * TPB * 6:(b + 1) * TPB * 6], mean2[:, at], var[:, at], half[:, at], EPS)

            over = lambda ap: ap.unsqueeze(1).broadcast_to((P, TPB, EXPERTS))
            te = lambda n: route[:, n * BE:(n + 1) * BE].rearrange("p (t e) -> p t e", e=EXPERTS)
            wide = lambda ap: ap.unsqueeze(2).broadcast_to((P, TPB, EXPERTS))
            per_tile = lambda n: topv[:, n * TPB:(n + 1) * TPB]
            four = lambda ap: ap.rearrange("p (n d) -> p n d", d=P)
            all4 = lambda ap: ap.unsqueeze(1).broadcast_to((P, WIDE, P))

            def hidden(b):
                dve.wait_ge(rstd_ready, BATCHES + 2 + b)
                for p in range(2):
                    g = 2 * b + p
                    for n in range(WIDE):
                        t = g * WIDE + n
                        last = v.tensor_scalar(hn[p][:, n * P:(n + 1) * P], cols(X, t), cols(mean2, t, 1),
                                               cols(rstd2, t, 1), ALU.subtract, ALU.mult)
                    last.then_inc(n2_ready, 1)
                for p in range(2):
                    dve.wait_ge(n2_ready, 2 * b + p + 1)
                    v.tensor_tensor(four(hn[p][:, :]), four(hn[p][:, :]), all4(cols(MOD, 4 * b + 2)), ALU.mult)\
                     .then_inc(m2_ready, 1)
                for p in range(2):
                    g = 2 * b + p
                    dve.wait_ge(m2_ready, g + 1)
                    need(dve, h2T_ready, g - 1)
                    need(dve, row_ready, TOP_K * (g - 1))
                    v.tensor_tensor(four(h2[p][:, :]), four(hn[p][:, :]), all4(cols(MOD, 4 * b + 1)), ALU.add)\
                     .then_inc(h2_ready, 1)

            def first_of_largest(logits, value, onehot):
                link(v.tensor_reduce(value, logits, AX.X, ALU.max))
                link(v.tensor_tensor(onehot, logits, wide(value), ALU.is_equal))
                link(v.tensor_tensor(onehot, onehot, over(const("rank")), ALU.mult))
                link(v.tensor_reduce(per_tile(2), onehot, AX.X, ALU.max))
                link(v.tensor_tensor(onehot, over(const("rank")), wide(per_tile(2)), ALU.is_equal))

            def router(b):
                dve.wait_ge(lg_ready, 2 * (b + 1))
                v.tensor_tensor(te(0), bank[4][:, 0:BE].rearrange("p (t e) -> p t e", e=EXPERTS), over(wgt("r_b")),
                                ALU.add).then_inc(lg_read, 1)
                dve.wait_ge(lg_read, b + 1)
                first_of_largest(te(0), per_tile(0), te(1))
                link(v.tensor_scalar(te(2), te(1), -3.0e38, None, ALU.mult))
                link(v.tensor_tensor(te(2), te(2), te(0), ALU.add))
                first_of_largest(te(2), per_tile(1), te(3))
                v.tensor_tensor(per_tile(2), per_tile(1), per_tile(0), ALU.subtract).then_inc(exp_in, 1)

                need(dve, rank_ready, b)
                v.tensor_copy(CHOSEN_BEFORE[:, 0:EXPERTS], CHOSEN_BEFORE[:, BE:])
                link(v.tensor_tensor(CHOSEN[:, :], route[:, BE:2 * BE], route[:, 3 * BE:4 * BE], ALU.add))
                for n in range(TPB):
                    ins = v.tensor_tensor(CHOSEN_BEFORE[:, (n + 1) * EXPERTS:(n + 2) * EXPERTS],
                                          CHOSEN_BEFORE[:, n * EXPERTS:(n + 1) * EXPERTS],
                                          CHOSEN[:, n * EXPERTS:(n + 1) * EXPERTS], ALU.add)
                    if n < TPB - 1:
                        link(ins)
                ins.then_inc(chosen_ready, 1)

                dve.wait_ge(exp_out, b + 1)
                at = [CHOICE[:, k * TILES + b * TPB:k * TILES + (b + 1) * TPB] for k in range(TOP_K)]
                link(v.tensor_scalar(per_tile(2), per_tile(3), 1.0, None, ALU.add))
                link(v.reciprocal(at[0], per_tile(2)))
                link(v.tensor_tensor(at[1], at[0], per_tile(3), ALU.mult))

                dve.wait_ge(rank_ready, b + 1)
                v.tensor_tensor(te(0), bank[5][:, 0:BE].rearrange("p (t e) -> p t e", e=EXPERTS),
                                over(const("region")), ALU.add).then_inc(rank_read, 1)
                dve.wait_ge(rank_read, b + 1)
                v.tensor_tensor(te(1), te(1), te(0), ALU.mult)
                link(v.tensor_tensor(te(3), te(3), te(0), ALU.mult))
                v.tensor_reduce(slotf[:, 0:TPB], te(1), AX.X, ALU.add)
                link(v.tensor_reduce(slotf[:, TPB:], te(3), AX.X, ALU.add))
                v.tensor_copy(SLOT[:, b * TOP_K * TPB:(b + 1) * TOP_K * TPB], slotf[:, :]).then_inc(slot_ready, 1)

            for k in range(TOP_K):
                dst = ROWS[k][:, :].rearrange("p (t d) -> p t d", d=ROW)[:, :, P]
                link(v.tensor_scalar(dst, const("token"), float(k * TOKENS), None, ALU.add))
            for b in range(BATCHES):
                hidden(b)
                router(b)

            dve.wait_ge(count_ready, 1)
            dve.wait_ge(plan_loaded, 16)
            at, work = 0, {}
            for name, n in [("count", EXPERTS), ("steps", EXPERTS), ("upto", EXPERTS), ("end", EXPERTS),
                            ("past", STEPS * EXPERTS), ("spent", STEPS * EXPERTS), ("expert", STEPS),
                            ("start", STEPS), ("used", STEPS), ("skip", STEPS), ("begun", EXPERTS * (TOKENS // SLOTS))]:
                work[name] = plan_w[:, at:at + n]
                at += n
            table = lambda name: PLAN[:, plan_at[name][0]:plan_at[name][1]]
            pairs = lambda ap, n: ap.rearrange("p (a b) -> p a b", b=n)
            per_row = lambda ap, n: ap.unsqueeze(2).broadcast_to((1, ap.shape[1], n))
            per_col = lambda ap, n: ap.unsqueeze(1).broadcast_to((1, n, ap.shape[1]))
            FS = TOKENS // SLOTS
            link(v.tensor_copy(work["count"], bank[6][0:1, 0:EXPERTS]))
            link(v.tensor_tensor(pairs(work["begun"], FS), per_row(work["count"], FS), pairs(table("fill"), FS),
                                 ALU.is_gt))
            link(v.tensor_reduce(work["steps"], pairs(work["begun"], FS), AX.X, ALU.add))
            upto = work["past"][:, 0:EXPERTS * EXPERTS]
            link(v.tensor_tensor(pairs(upto, EXPERTS), pairs(table("upto"), EXPERTS), per_col(work["steps"], EXPERTS),
                                 ALU.mult))
            link(v.tensor_reduce(work["upto"], pairs(upto, EXPERTS), AX.X, ALU.add))
            link(v.tensor_tensor(pairs(work["past"], EXPERTS), pairs(table("step"), EXPERTS),
                                 per_col(work["upto"], STEPS), ALU.is_ge))
            link(v.tensor_tensor(pairs(work["spent"], EXPERTS), pairs(work["past"], EXPERTS),
                                 per_col(work["steps"], STEPS), ALU.mult))
            link(v.tensor_reduce(work["expert"], pairs(work["past"], EXPERTS), AX.X, ALU.add))
            link(v.tensor_reduce(work["skip"], pairs(work["spent"], EXPERTS), AX.X, ALU.add))
            link(v.tensor_tensor(work["start"], table("index"), work["skip"], ALU.subtract))
            link(v.tensor_scalar(work["used"], work["expert"], EXPERTS - 0.5, float(SLOTS), ALU.is_lt, ALU.mult))
            link(v.tensor_tensor(work["start"], work["start"], work["used"], ALU.mult))
            link(v.scalar_tensor_tensor(out=work["start"], in0=work["expert"], scalar=float(REGION), in1=work["start"],
                                        op0=ALU.mult, op1=ALU.add))
            link(v.tensor_scalar(work["expert"], work["expert"], float(EXPERTS - 1), None, ALU.min))
            link(v.tensor_tensor(work["end"], work["count"], table("start"), ALU.add))
            v.tensor_copy(STEP_START[:, :], work["start"]).then_inc(plan_ready, 1)
            v.tensor_copy(STEP_EXPERT[:, :], work["expert"]).then_inc(plan_ready, 1)
            v.tensor_copy(FILLED[:, :], work["end"]).then_inc(plan_ready, 1)

            y4 = YT[:, :].rearrange("p (b t d) -> p b t d", b=BATCHES, d=P)
            x4 = X[:, :].rearrange("p (b t d) -> p b t d", b=BATCHES, d=P)
            for b in range(BATCHES):
                link(v.tensor_tensor(y4[:, b], x4[:, b], cols(LNB, b).unsqueeze(1).broadcast_to((P, TPB, P)), ALU.add))

            def take_rows(r):
                p = r % 2
                v.tensor_copy(INT[p][:, :], bank[4 + p][:, 0:SLOTS]).then_inc(inT_ready, 1)

            def take_dest(i, r):
                p = r % 2
                need(dve, sent_back[p], (i - p) * 8 * NS)
                v.tensor_copy(DEST[p][:, :], IN[r][:, :].rearrange("p (n d) -> p n d", d=ROW)[:, :, P])\
                 .then_inc(dest_ready, 1)
                need(dve, moe_ready, i + 1)
                v.tensor_tensor(RES[p][:, :].rearrange("p (n d) -> p n d", d=P),
                                bank[6 + p][:, 0:SLOTS].rearrange("p (n d) -> p n d", d=P),
                                EW[r][:, FF + FC * P + FC:].unsqueeze(1).broadcast_to((P, NS, P)), ALU.add)\
                 .then_inc(res_ready, 1)

            def c_step(i, r):
                if not (isinstance(i, int) and i == STEPS - 1):
                    need(dve, inT_ps, i + 2)
                    need(dve, hid_ps, FC * i)
                    take_rows((r + 1) % RING)
                take_dest(i, r)

            dve.wait_ge(inT_ps, 1)
            take_rows(0)
            expert_loop(dve, c_step)

            def row(t):
                at = t * ROW
                return ROWS[0][:, at:at + P] if isinstance(t, int) else ROWS[0][:, bass.ds(at, P)]

            def add_results(g, p):
                need(dve, back_loaded[p], 16 * TOP_K * ((g - p) // 2 + 1) if isinstance(g, int) else (g - p) * 16 + 32)
                need(dve, sum_b, WIDE * g)
                for k, done in enumerate((sum_a, sum_b)):
                    if k:
                        need(dve, sum_a, WIDE * (g + 1))
                    for n in range(WIDE):
                        t = g * WIDE + n
                        w = CHOICE[:, k * TILES:(k + 1) * TILES]
                        v.scalar_tensor_tensor(out=row(t), in0=BACK[p][:, (k * WIDE + n) * P:(k * WIDE + n + 1) * P],
                                               scalar=cols(w, t, 1), in1=row(t), op0=ALU.mult, op1=ALU.add)\
                         .then_inc(done, 1)
                    if k == 0 and not (isinstance(g, int) and g == 0):
                        sums_stats(g - 1)

            def sums_stats(g):
                for n in range(WIDE):
                    t = g * WIDE + n
                    v.bn_stats(cols(fstat, t, 6), row(t)).then_inc(fstat_ready, 1)

            group_loop(dve, add_results)
            dve.wait_ge(sum_b, TILES)
            sums_stats(TILES // WIDE - 1)
            dve.wait_ge(fstat_ready, TILES)
            moments(fstat[:, :], mean1[:, :], var[:, :], half[:, :], EPS_FFN)
            dve.wait_ge(rstd_ready, 2 * BATCHES + 2)
            v.scalar_tensor_tensor(out=mean1[:, :], in0=mean1[:, :], scalar=-1.0, in1=rstd1[:, :], op0=ALU.mult,
                                   op1=ALU.mult).then_inc(last_ready, 1)

            def finish(g, p):
                b = g // 2
                need(dve, fin_a, g + 1)
                v.tensor_tensor(four(fin[p][:, :]), four(fin[p][:, :]), all4(cols(LNW, b)), ALU.mult).then_inc(fin_b, 1)
                need(dve, fin_b, g + 1)
                y = YT[:, g * WIDE * P:(g + 1) * WIDE * P] if isinstance(g, int) else \
                    YT[:, bass.ds(g * (WIDE * P), WIDE * P)]
                v.tensor_tensor(fin[p][:, :], fin[p][:, :], y, ALU.add).then_inc(fin_ready, 1)

            group_loop(dve, finish)


def kernel(**inputs):
    import concourse.bacc as _bacc
    from concourse.bass_utils import run_bass_kernel_spmd as _run

    def arr(name):
        return np.ascontiguousarray(inputs[name])

    def rows(name):
        return np.tile(arr(name)[None, :], (P, 1))

    parts = {
        "wqT": arr("L0_attn_W_q").T, "wkT": arr("L0_attn_W_k").T, "wvT": arr("L0_attn_W_v").T,
        "wkT2": arr("L0_attn_W_k").T, "woT": arr("L0_attn_W_o").T, "wmod": arr("L0_wmod"), "cT": arr("L0_c").T,
        "gn_w": arr("L0_attn_gn_weight")[:, None], "gn_b": arr("L0_attn_gn_bias")[:, None],
        "rwT": arr("L0_ffn_router_w").T, "r_b": rows("L0_ffn_router_b"),
        "ln_w": rows("L0_ffn_ln_w"), "ln_b": rows("L0_ffn_ln_b"),
    }
    w1, w2, b1 = arr("L0_ffn_w1"), arr("L0_ffn_w2"), arr("L0_ffn_b1")
    experts = np.concatenate([
        w1.transpose(0, 2, 1),
        w2.transpose(0, 2, 1).reshape(EXPERTS, FC, P, P).transpose(0, 2, 1, 3).reshape(EXPERTS, P, FC * P),
        b1.reshape(EXPERTS, FC, P).transpose(0, 2, 1),
        np.broadcast_to(arr("L0_ffn_b2")[:, None, :], (EXPERTS, P, P))], axis=2)
    arrays = {
        "x": arr("L0_attn_x"),
        "weights": np.concatenate([parts[n] for n, _ in WEIGHTS], axis=1),
        "consts": np.concatenate(list(shape_constants().values()), axis=1),
        "experts": experts,
        "plan": np.concatenate(list(plan_tables().values()))[None, :],
    }
    arrays = {k: np.ascontiguousarray(a) for k, a in arrays.items()}
    nc = _bacc.Bacc("TRN2", target_bir_lowering=False, num_devices=1)
    args = [nc.dram_tensor(k, a.shape, mybir.dt.from_np(a.dtype), kind="ExternalInput").ap() for k, a in arrays.items()]
    args.append(nc.dram_tensor("out", arrays["x"].shape, F32, kind="ExternalOutput").ap())
    build(nc, *args)
    return _run(nc, [arrays], core_ids=[0]).results[0]["out"]
```

```python
from contextlib import ExitStack

import numpy as np

import concourse.bass as bass
from concourse import mybir

F32 = mybir.dt.float32
F32R = mybir.dt.float32r
I32 = mybir.dt.int32
ACT = mybir.ActivationFunctionType
ALU = mybir.AluOpType
AX = mybir.AxisListType

P = 128
HEADS = 16
DH = P // HEADS
BATCHES = 4
SEQ = 1024
TILES = BATCHES * SEQ // P
TPB = SEQ // P
C = 64
CPT = P // C
GROUPS = 4
HPG = HEADS // GROUPS
HALF = HEADS // 2
POOL_HEADS = 10
LANE = 64 + DH
EXPERTS = 8
FF = 512
FC = FF // P
TOKENS = TILES * P
TOP_K = 2
SLOTS = 256
NS = SLOTS // P
REGION = TOKENS + SLOTS
NOWHERE = 8 * TOKENS
ROW = P + 2
WIDE = 4
RING = 4
STEPS = TOP_K * TOKENS // SLOTS + EXPERTS - 1
ROUNDS = -(-STEPS // RING)
LAST_ROUND = STEPS - RING * (ROUNDS - 1)
EPS = 1e-5
EPS_FFN = 1e-12


STAGES = 16
AFTER_TILES = [(3, 0), (2, 8), (3, 1), (3, 2), (2, 9), (3, 3), (3, 4), (3, 5), (2, 10), (3, 6), (2, 11), (2, 12),
               (3, 7), (2, 13), (3, 8), (2, 14), (3, 9), (2, 15), (3, 10), (3, 11), (3, 12), (3, 13), (3, 14), (3, 15)]
PEELED = 2


def shape_constants():
    gamma = 1.0 - 2.0 ** (-5.0 - np.arange(HEADS, dtype=np.float64))
    head = np.arange(P) // DH
    j, i = np.arange(C)[:, None], np.arange(C)[None, :]
    decay = np.where(i >= j, gamma[:, None, None] ** np.maximum(i - j, 0), 0.0) / np.sqrt(DH)
    decay = np.tile(decay.transpose(1, 0, 2).reshape(C, HEADS * C), (CPT, 1))
    qdec = np.tile(gamma[head][:, None] ** (i + 1) / np.sqrt(DH), (1, CPT))
    chunk = np.arange(TILES * CPT)
    tables = {
        "ident": np.eye(P),
        "same_head": (head[:, None] == head[None, :]),
        "head_mean": (head[:, None] == head[None, :]) / DH,
        "qdec": qdec,
        "qdec_first": np.where(np.arange(P)[None, :] < C, 0.0, qdec),
        "kdec": np.tile(gamma[head][None, :] ** (C - 1 - j), (CPT, 1)),
        "of_head": (head[:, None] == np.arange(HEADS)[None, :]),
        "carry": np.where(chunk[None, :] % (TPB * CPT) == 0, 0.0, gamma[head][:, None] ** C),
        "before": (np.arange(P)[:, None] < np.arange(P)[None, :]),
        "ones": np.ones((P, P)),
        "region": np.tile(REGION * np.arange(EXPERTS)[None, :], (P, 1)),
        "token": np.arange(P)[:, None] + P * np.arange(TILES)[None, :],
        "rank": np.tile(np.arange(EXPERTS, 0, -1.0)[None, :], (P, 1)),
        "decay": decay,
    }
    return {k: np.ascontiguousarray(v, np.float32) for k, v in tables.items()}


def plan_tables():
    e = np.arange(EXPERTS)
    tables = {
        "fill": np.tile(SLOTS * np.arange(TOKENS // SLOTS), EXPERTS),
        "upto": (e[None, :] <= e[:, None]).ravel(),
        "step": np.repeat(np.arange(STEPS), EXPERTS),
        "index": np.arange(STEPS),
        "start": REGION * e,
    }
    return {k: np.ascontiguousarray(v, np.float32) for k, v in tables.items()}


WEIGHTS = [("wqT", P), ("wkT", P), ("wvT", P), ("wkT2", P), ("woT", P), ("wmod", 6 * P), ("cT", BATCHES),
           ("gn_w", 1), ("gn_b", 1), ("rwT", EXPERTS), ("r_b", EXPERTS), ("ln_w", P), ("ln_b", P)]
EXPERT_COLS = FF + FC * P + FC + P


def offsets(widths):
    at, out = 0, {}
    for name, n in widths:
        out[name] = (at, at + n)
        at += n
    return out, at


def build(nc, x, weights, consts, experts, plan, out):
    const_at, const_cols = offsets([(k, v.shape[1]) for k, v in shape_constants().items()])
    weight_at, weight_cols = offsets(WEIGHTS)
    plan_at, plan_cols = offsets([(k, len(v)) for k, v in plan_tables().items()])
    dispatch = nc.dram_tensor("dispatch", (EXPERTS * REGION + SLOTS, ROW), F32).ap()
    returned = nc.dram_tensor("returned", (TOP_K * TOKENS, P), F32).ap()

    with ExitStack() as ctx:
        def sb(name, cols, parts=P, dtype=F32):
            return ctx.enter_context(nc.sbuf_tensor(name, [parts, cols], dtype))

        def sem(name):
            return ctx.enter_context(nc.semaphore(name))

        CONST = sb("CONST", const_cols)
        WGT = sb("WGT", weight_cols)

        def const(name):
            return CONST[:, const_at[name][0]:const_at[name][1]]

        def wgt(name):
            return WGT[:, weight_at[name][0]:weight_at[name][1]]

        X = sb("X", TILES * P)
        YT = sb("YT", TILES * P)
        ROWS = [sb(f"ROWS_{k}", TILES * ROW) for k in range(TOP_K)]
        stat = sb("stat", TILES * 6)
        ystat = sb("ystat", TILES * 6)
        xstat = sb("xstat", TILES * 6)
        mean1, rstd1 = sb("mean1", TILES), sb("rstd1", TILES)
        mean2, rstd2 = sb("mean2", TILES), sb("rstd2", TILES)
        var = sb("var", TILES)
        half = sb("half", TILES)
        minus_half = sb("minus_half", TILES)
        silu = sb("silu", 3 * BATCHES)
        silu_bc = sb("silu_bc", BATCHES * P)
        shiftT, scaleT = sb("shiftT", TILES), sb("scaleT", TILES)
        MOD = sb("MOD", BATCHES * 4 * P)
        gate = sb("gate", 2 * BATCHES * P)
        WOG = sb("WOG", BATCHES * P)
        LNW, LNB = sb("LNW", BATCHES * P), sb("LNB", BATCHES * P)
        gn = sb("gn", 2 * BATCHES)
        gsc = sb("gsc", 4 * BATCHES)

        h0 = [sb(f"h0_{p}", P) for p in range(2)]
        hT = [sb(f"hT_{p}", P) for p in range(2)]
        QK = [sb(f"QK_{p}", 2 * P) for p in range(2)]
        Qm = [sb(f"Qm_{p}", HEADS * P) for p in range(2)]
        Qd = [sb(f"Qd_{p}", P) for p in range(2)]
        V = [sb(f"V_{p}", GROUPS * HPG * LANE) for p in range(2)]
        Kd = [sb(f"Kd_{p}", P) for p in range(2)]
        PR = [sb(f"PR_{p}", HEADS * C) for p in range(2)]
        UM = sb("UM", CPT * P)
        STATE = [sb(f"STATE_{n}", GROUPS * 64) for n in range(2 * CPT)]
        yn = [sb(f"yn_{g}", WIDE * P) for g in range(2)]
        hn = [sb(f"hn_{g}", WIDE * P) for g in range(2)]
        h2 = [sb(f"h2_{g}", WIDE * P) for g in range(2)]
        h2t = [sb(f"h2t_{g}", WIDE * P) for g in range(2)]
        BE = TPB * EXPERTS
        route = sb("route", 4 * BE)
        CHOSEN = [sb(f"CHOSEN_{n}", 2 * BE) for n in range(4)]
        CHOSEN_BEFORE = sb("CHOSEN_BEFORE", EXPERTS)
        topv = sb("topv", 4 * TPB)
        slotf = sb("slotf", TOP_K * TPB)
        SLOT = sb("SLOT", TOP_K * TILES, dtype=I32)
        PLAN = sb("PLAN", plan_cols, 1)
        plan_w = gate[0:1, :]
        STEP_START = sb("STEP_START", STEPS, 1, I32)
        STEP_EXPERT = sb("STEP_EXPERT", STEPS, 1, I32)
        FILLED = sb("FILLED", EXPERTS, 1, I32)
        PADDING = sb("PADDING", NS * ROW)
        IN = [sb(f"IN_{r}", NS * ROW) for r in range(RING)]
        EW = [sb(f"EW_{r}", EXPERT_COLS) for r in range(RING)]
        DEST = [sb(f"DEST_{p}", NS, dtype=I32) for p in range(2)]
        ROW_HI = [sb(f"ROW_HI_{p}", SLOTS, dtype=F32R) for p in range(2)]
        ROW_LO = [sb(f"ROW_LO_{p}", SLOTS, dtype=F32R) for p in range(2)]
        W1_HI = [sb(f"W1_HI_{p}", FF, dtype=F32R)[:, :] for p in range(2)]
        W1_LO = [sb(f"W1_LO_{p}", FF, dtype=F32R)[:, :] for p in range(2)]
        HID = [yn[f // 2][:, f % 2 * SLOTS:(f % 2 + 1) * SLOTS] for f in range(FC)]
        RES = [h2[p][:, 0:SLOTS] for p in range(2)]
        tick = sb("tick", 2)
        BACK = [buffer[:, 0:TOP_K * WIDE * P] for buffer in PR + V]
        fin = [Qm[g // 4][:, g % 4 * WIDE * P:(g % 4 + 1) * WIDE * P] for g in range(TILES // WIDE)]
        fstat = sb("fstat", TILES * 6)

        bank = [ctx.enter_context(nc.psum_tensor(f"bank{n}", [P, 512], F32)) for n in range(8)]
        BB, QB, KB, YB = bank[0], bank[1], bank[2], bank[3]
        TB, GM = QB[:, 2 * P:3 * P], QB[:, 3 * P:3 * P + 2]
        SC = bank[4:8]
        SIDE = [BB] * (BATCHES - 1) + [SC[3]]

        x_loaded = [sem(f"x_loaded{b}") for b in range(BATCHES)]
        decay_loaded, gm_read = sem("decay_loaded"), sem("gm_read")
        const_loaded, wgt_loaded = sem("const_loaded"), sem("wgt_loaded")
        dve_chain, act_step, pool_step, silu_ready = sem("dve_chain"), sem("act_step"), sem("pool_step"), sem("silu_ready")
        tick_done = sem("tick_done")
        var_ready, rstd_ready = sem("var_ready"), sem("rstd_ready")
        mod_ready, mod_read = sem("mod_ready"), sem("mod_read")
        h0_ready, h0T_ready, hT_ready = sem("h0_ready"), sem("h0T_ready"), sem("hT_ready")
        qk_ps, qk_ready, kv_ready, qm_ready = sem("qk_ps"), sem("qk_ready"), sem("kv_ready"), sem("qm_ready")
        qm2_ready = sem("qm2_ready")
        kvs_ready, qd_ready = sem("kvs_ready"), sem("qd_ready")
        sc_ready, p_ready = sem("sc_ready"), sem("p_ready")
        u_ready, um_ready, s_ready = sem("u_ready"), sem("um_ready"), sem("s_ready")
        y_ready, YT_ready = sem("y_ready"), sem("YT_ready")
        ystat_ready = sem("ystat_ready")
        gmean_ready, gm_ready, gn_ready = sem("gmean_ready"), sem("gm_ready"), sem("gn_ready")
        yn_ready, att_ready, x2_ready = sem("yn_ready"), sem("att_ready"), sem("x2_ready")
        n2_ready, m2_ready, h2_ready = sem("n2_ready"), sem("m2_ready"), sem("h2_ready")
        h2T_ready, h2t_ready, lg_ready, lg_read = sem("h2T_ready"), sem("h2t_ready"), sem("lg_ready"), sem("lg_read")
        row_ready, exp_in, exp_out = sem("row_ready"), sem("exp_in"), sem("exp_out")
        chosen_ready, rank_ready, rank_read = sem("chosen_ready"), sem("rank_ready"), sem("rank_read")
        slot_ready, scattered, padded = sem("slot_ready"), sem("scattered"), sem("padded")
        plan_loaded, count_ready, plan_ready = sem("plan_loaded"), sem("count_ready"), sem("plan_ready")
        in_loaded = [sem(f"in_loaded{r}") for r in range(RING)]
        ew_loaded = [sem(f"ew_loaded{r}") for r in range(RING)]
        inT_ps, inT_ready, dest_ready = sem("inT_ps"), sem("inT_ready"), sem("dest_ready")
        hid_ps, hid_ready, moe_ready, res_ready = sem("hid_ps"), sem("hid_ready"), sem("moe_ready"), sem("res_ready")
        sum_ready, w1_hi, w1_lo, row_hi = sem("sum_ready"), sem("w1_hi"), sem("w1_lo"), sem("row_hi")
        sent_back = [sem(f"sent_back{p}") for p in range(2)]
        back_loaded = [sem(f"back_loaded{r}") for r in range(4)]
        total_ready = sem("total_ready")
        shift2_ready = sem("shift2_ready")
        sum_ps, shift_ready = sem("sum_ps"), sem("shift_ready")
        fin_a, fin_b, fin_ready, fin_late = sem("fin_a"), sem("fin_b"), sem("fin_ready"), sem("fin_late")
        stored = sem("stored")
        BY_POOL = TILES // WIDE - 2

        block = ctx.enter_context(nc.Block())

        def need(eng, s, value):
            if isinstance(value, int) and value <= 0:
                return
            eng.wait_ge(s, value)

        def phases_a_b(eng, step, stage, early=None):
            def peeled(t, n):
                step(t, t % 2)
                if early:
                    early(n)

            for t in range(PEELED):
                peeled(t, t)
            with eng.Fori(PEELED // 2, (TPB - PEELED) // 2) as pair:
                step(2 * pair, 0)
                step(2 * pair + 1, 1)
            for t in range(TPB - PEELED, TPB):
                peeled(t, t - TPB + 2 * PEELED)
            for t in range(TPB, TILES):
                step(t, t % 2)
                if stage:
                    stages(stage, t)
            if stage:
                remaining_stages(stage)

        def stages(stage, t):
            if isinstance(t, int):
                for b in range(BATCHES):
                    if 0 <= t - TPB * (b + 1) < STAGES:
                        stage(b, t - TPB * (b + 1))

        def remaining_stages(*kinds):
            for b, s in AFTER_TILES:
                for stage in kinds:
                    stage(b, s)

        def expert_loop(eng, step):
            for r in range(RING):
                step(r, r)
            with eng.Fori(1, ROUNDS - 1) as turn:
                for r in range(RING):
                    step(RING * turn + r, r)
            for r in range(LAST_ROUND):
                step(RING * (ROUNDS - 1) + r, r)

        def cols(tensor, t, n=P):
            return tensor[:, t * n:(t + 1) * n] if isinstance(t, int) else tensor[:, bass.ds(t * n, n)]

        def last_tile(t):
            return isinstance(t, int) and t == TILES - 1

        def near_end(t):
            return isinstance(t, int) and t >= TILES - 2

        @block.sync
        def _(sp):
            x_v = x.rearrange("b (n p) d -> p b n d", p=P)
            sp.dma_start(WGT[:, :], weights).then_inc(wgt_loaded, 16)
            small = const_at["decay"][0]
            for b in range(BATCHES):
                sp.dma_start(X[:, b * SEQ:(b + 1) * SEQ].rearrange("p (n d) -> p n d", d=P), x_v[:, b])\
                  .then_inc(x_loaded[b], 16)
                if b == 0:
                    sp.dma_start(CONST[:, 0:small], consts[:, 0:small]).then_inc(const_loaded, 16)
                    sp.dma_start(CONST[:, small:], consts[:, small:]).then_inc(decay_loaded, 16)
            sp.dma_start(PLAN[:, :], plan).then_inc(plan_loaded, 16)

            def load_weights(i, r):
                need(sp, res_ready, i - RING + 1)
                e = sp.value_load(cols(STEP_EXPERT, i, 1), min_val=0, max_val=EXPERTS - 1)
                sp.dma_start(EW[r][:, :], experts[bass.ds(e, 1)].rearrange("a p n -> p (a n)")).then_inc(ew_loaded[r], 16)

            def load_rows(i, r):
                start = sp.value_load(cols(STEP_START, i, 1), min_val=0, max_val=EXPERTS * REGION)
                if isinstance(i, int) and i == 0:
                    sp.wait_ge(padded, 16 * (EXPERTS + 1))
                    sp.wait_ge(scattered, 16 * TOP_K * TILES)
                sp.dma_start(IN[r][:, :].rearrange("p (n d) -> p n d", d=ROW),
                             dispatch[bass.ds(start, SLOTS), :].rearrange("(n p) d -> p n d", p=P))\
                  .then_inc(in_loaded[r], 16)

            def load_step(i, r):
                if not (isinstance(i, int) and i < RING):
                    load_weights(i, r)
                load_rows(i, r)

            sp.wait_ge(plan_ready, 3)
            for r in range(RING):
                load_weights(r, r)
            expert_loop(sp, load_step)

            for p in range(2):
                sp.wait_ge(sent_back[p], 16 * NS * ((STEPS + 1 - p) // 2))
            back_v = returned.rearrange("(k g n p) d -> g p k n d", k=TOP_K, n=WIDE, p=P)
            out_v = out.rearrange("b (g n p) d -> (b g) p n d", n=WIDE, p=P)

            def load_back(g):
                need(sp, sum_ps, g - 3)
                dst = BACK[g % 4].rearrange("p (k n d) -> p k n d", k=TOP_K, d=P)
                for k in range(TOP_K):
                    sp.dma_start(dst[:, k], back_v[g][:, k]).then_inc(back_loaded[g % 4], 16)

            def store(g):
                if g < BY_POOL:
                    sp.wait_ge(fin_ready, g + 1)
                else:
                    sp.wait_ge(fin_late, g + 1 - BY_POOL)
                sp.dma_start(out_v[g], fin[g].rearrange("p (n d) -> p n d", d=P)).then_inc(stored, 16)

            for g in range(TILES // WIDE):
                load_back(g)
            for g in range(TILES // WIDE):
                store(g)
            sp.wait_ge(stored, 16 * TILES // WIDE)

        @block.gpsimd
        def _(pool):
            nc.gpsimd.memset(minus_half[:, :], -0.5).then_inc(pool_step, 1)
            for n in range(2 * CPT):
                nc.gpsimd.memset(STATE[n][:, :], 0.0).then_inc(pool_step, 1)
            nc.gpsimd.memset(CHOSEN_BEFORE[:, :], 0.0).then_inc(pool_step, 1)
            for n in range(4):
                nc.gpsimd.memset(CHOSEN[n][:, :], 0.0).then_inc(pool_step, 1)
            nc.gpsimd.memset(tick[:, :], 0.0).then_inc(pool_step, 1)
            nc.gpsimd.memset(PADDING[:, :], 0.0).then_inc(pool_step, 1)
            pool.wait_ge(pool_step, 12)
            for p in range(2):
                nc.gpsimd.memset(V[p][:, :], 0.0).then_inc(pool_step, 1)
            pad = PADDING[:, :].rearrange("p (n d) -> p n d", d=ROW)
            nc.gpsimd.memset(pad[:, :, P:ROW], float(NOWHERE)).then_inc(pool_step, 1)
            step = [0]

            def rsqrt(dst, src):
                step[0] += 1
                pool.wait_ge(var_ready, step[0])
                n = dst.shape[1]
                nc.gpsimd.tensor_tensor(dst, src, minus_half[:, 0:n], ALU.pow).then_inc(rstd_ready, 1)

            def rsqrt_tiles(dst, b):
                at = slice(b * TPB, (b + 1) * TPB)
                rsqrt(dst[:, at], var[:, at])

            rsqrt_tiles(rstd1, 0)

            def queries(u, p):
                need(pool, qk_ready, u + 1)
                need(pool, sc_ready, 2 * (u - 1))
                nc.gpsimd.tensor_tensor(Qm[p][:, 0:POOL_HEADS * P].rearrange("p (h i) -> p h i", i=P),
                                        QK[p][:, 0:P].unsqueeze(1).broadcast_to((P, POOL_HEADS, P)),
                                        const("of_head")[:, 0:POOL_HEADS].unsqueeze(2)
                                        .broadcast_to((P, POOL_HEADS, P)), ALU.mult).then_inc(qm_ready, 1)
                need(pool, y_ready, u - 1)
                first = isinstance(u, int) and u % TPB == 0
                nc.gpsimd.tensor_tensor(Qd[p][:, :], QK[p][:, 0:P], const("qdec_first" if first else "qdec"),
                                        ALU.mult).then_inc(qd_ready, 1)

            def a_step(t, p):
                if not last_tile(t):
                    queries(t + 1, 1 - p)

            def early(n):
                if n + 1 < BATCHES:
                    rsqrt_tiles(rstd1, n + 1)

            def b_stage(b, s):
                if s == 1:
                    rsqrt(gsc[:, 4 * b + 3:4 * b + 4], gsc[:, 4 * b + 2:4 * b + 3])
                if s == 5:
                    rsqrt_tiles(rstd2, b)
                    pool.wait_ge(rstd_ready, BATCHES + 2 * b + 2)
                    at = slice(b * TPB, (b + 1) * TPB)
                    nc.gpsimd.tensor_tensor(mean2[:, at], mean2[:, at], rstd2[:, at], ALU.mult).then_inc(shift2_ready, 1)
                if s >= 12:
                    if s == 12:
                        pool.wait_ge(slot_ready, b + 1)
                        pool.wait_ge(row_ready, 2 * TOP_K * (b + 1))
                    for n in range((s - 12) * TPB // 4, (s - 11) * TPB // 4):
                        t = b * TPB + n
                        for k in range(TOP_K):
                            at = (b * TOP_K + k) * TPB + n
                            nc.gpsimd.indirect_dma_start(
                                dispatch, bass.IndirectOffsetOnAxis(SLOT[:, at:at + 1], 0),
                                ROWS[k][:, t * ROW:(t + 1) * ROW], None).then_inc(scattered, 16)

            pool.wait_ge(const_loaded, 16)
            queries(0, 0)
            phases_a_b(pool, a_step, b_stage, early)

            def send_back(i, r):
                p = r % 2
                need(pool, tick_done, i)
                need(pool, res_ready, i + 1)
                nc.gpsimd.tensor_tensor(tick[:, 0:1], tick[:, 1:2], tick[:, 1:2], ALU.add).then_inc(tick_done, 1)
                for n in range(NS):
                    nc.gpsimd.indirect_dma_start(
                        returned, bass.IndirectOffsetOnAxis(DEST[p][:, n:n + 1], 0),
                        RES[p][:, n * P:(n + 1) * P], None,
                        bounds_check=TOP_K * TOKENS - 1, oob_is_err=False).then_inc(sent_back[p], 16)

            expert_loop(pool, send_back)

            def add_residual(g):
                pool.wait_ge(fin_b, g + 1)
                nc.gpsimd.tensor_tensor(fin[g], fin[g], YT[:, g * WIDE * P:(g + 1) * WIDE * P], ALU.add)\
                    .then_inc(fin_ready, 1)

            for b in range(BATCHES):
                rsqrt_tiles(rstd1, b)
                if b:
                    add_residual(2 * b - 2)
                    add_residual(2 * b - 1)

        @block.scalar
        def _(act):
            act.wait_ge(wgt_loaded, 16)
            nc.scalar.activation(silu[:, 0:BATCHES], wgt("cT"), ACT.Exp, scale=-1.0).then_inc(act_step, 1)

            def front(u, p):
                need(act, h0T_ready, u + 1)
                need(act, kv_ready, u - 1)
                nc.scalar.activation(hT[p][:, :], TB[:, 0:P], ACT.Identity, bias=cols(shiftT, u, 1),
                                     scale=cols(scaleT, u, 1)).then_inc(hT_ready, 1)

            def queries_keys(u, p):
                need(act, qk_ps, u + 1)
                need(act, sc_ready, 2 * (u - 1))
                need(act, qd_ready, u - 1)
                nc.scalar.activation(QK[p][:, :], QB[:, 0:2 * P], ACT.Copy).then_inc(qk_ready, 1)
                need(act, qk_ready, u + 1)
                for h in range(POOL_HEADS, HEADS):
                    last = nc.scalar.activation(Qm[p][:, h * P:(h + 1) * P], QK[p][:, 0:P], ACT.Copy,
                                                scale=const("of_head")[:, h:h + 1])
                last.then_inc(qm2_ready, 1)

            def y_back(t):
                need(act, y_ready, t + 1)
                for g in range(GROUPS):
                    for c in range(CPT):
                        src = YB[64 * (g % 2) + 32 * c:64 * (g % 2) + 32 * (c + 1), g // 2 * C:(g // 2 + 1) * C]
                        dst = cols(YT[32 * g:32 * (g + 1), :], 2 * t + c, C)
                        last = nc.scalar.activation(dst, src, ACT.Copy)
                last.then_inc(YT_ready, 1)

            def step(t, p):
                stages(b_first, t)
                if not last_tile(t):
                    queries_keys(t + 1, 1 - p)
                stages(b_stage, t)
                if not near_end(t):
                    front(t + 2, p)
                stages(b_last, t)
                y_back(t)

            def norm_y(g, b):
                act.wait_ge(gn_ready, b + 1)
                need(act, att_ready, g - 1)
                for n in range(WIDE):
                    last = nc.scalar.activation(yn[g % 2][:, n * P:(n + 1) * P], cols(YT, g * WIDE + n), ACT.Identity,
                                                bias=gsc[:, 4 * b:4 * b + 1], scale=gsc[:, 4 * b + 3:4 * b + 4])
                last.then_inc(yn_ready, 1)

            def normalise_x2(b, p):
                act.wait_ge(shift2_ready, b + 1)
                need(act, h2_ready, 2 * (b - 1) + p + 1)
                for n in range(WIDE):
                    t = b * TPB + p * WIDE + n
                    last = nc.scalar.activation(hn[p][:, n * P:(n + 1) * P], cols(X, t), ACT.Identity,
                                                bias=cols(mean2, t, 1), scale=cols(rstd2, t, 1))
                last.then_inc(n2_ready, 1)

            def h2_back(g, p):
                act.wait_ge(h2T_ready, g + 1)
                need(act, lg_ready, g // 2)
                nc.scalar.activation(h2t[p][:, :], SIDE[g // 2][:, :], ACT.Copy).then_inc(h2t_ready, 1)

            def row_copies(g, p):
                for k in range(TOP_K):
                    dst = ROWS[k][:, g * WIDE * ROW:(g + 1) * WIDE * ROW].rearrange("p (n d) -> p n d", d=ROW)
                    nc.scalar.activation(dst[:, :, 0:P], h2[p][:, :].rearrange("p (n d) -> p n d", d=P), ACT.Copy)\
                        .then_inc(row_ready, 1)

            def b_first(b, s):
                if s in (8, 9):
                    h2_back(2 * b + s - 8, s - 8)
                if s == 11:
                    act.wait_ge(exp_in, b + 1)
                    nc.scalar.activation(topv[:, 3 * TPB:4 * TPB], topv[:, 2 * TPB:3 * TPB], ACT.Exp)\
                        .then_inc(exp_out, 1)

            def b_stage(b, s):
                if s in (3, 4):
                    norm_y(2 * b + s - 3, b)
                if s in (6, 7):
                    normalise_x2(b, s - 6)
                if s in (8, 9):
                    row_copies(2 * b + s - 8, s - 8)

            def b_last(b, s):
                if s == 1:
                    act.wait_ge(gm_ready, b + 1)
                    nc.scalar.activation(gsc[:, 4 * b:4 * b + 2], GM, ACT.Copy).then_inc(gm_read, 1)

            act.wait_ge(const_loaded, 16)
            act.wait_ge(mod_read, 2)
            front(0, 0)
            queries_keys(0, 0)
            front(1, 1)
            phases_a_b(act, step, None)
            remaining_stages(b_last, b_first, b_stage)

            padding = PADDING[:, :].rearrange("p (n d) -> p n d", d=ROW)
            act.wait_ge(plan_ready, 1)
            for e in range(EXPERTS):
                end = act.value_load(FILLED[0:1, e:e + 1], min_val=e * REGION, max_val=e * REGION + TOKENS)
                act.dma_start(dispatch[bass.ds(end, SLOTS), :].rearrange("(n p) d -> p n d", p=P), padding)\
                   .then_inc(padded, 16)
            act.dma_start(dispatch[EXPERTS * REGION:, :].rearrange("(n p) d -> p n d", p=P), padding)\
               .then_inc(padded, 16)

            def split_w1(i, r):
                act.wait_ge(ew_loaded[r], (i - r) * (16 // RING) + 16)
                need(act, hid_ps, (i - 1) * FC)
                nc.scalar.activation(W1_HI[r % 2], EW[r][:, 0:FF], ACT.Copy).then_inc(w1_hi, 1)

            def gelu(i, r):
                if not (isinstance(i, int) and i == STEPS - 1):
                    split_w1(i + 1, (r + 1) % RING)
                for f in range(FC):
                    need(act, hid_ps, i * FC + f + 1)
                    if f == 0:
                        need(act, moe_ready, i)
                    nc.scalar.activation(HID[f][:, :], bank[f][:, 0:SLOTS], ACT.Gelu,
                                         bias=EW[r][:, FF + FC * P + f:FF + FC * P + f + 1]).then_inc(hid_ready, 1)

            split_w1(0, 0)
            expert_loop(act, gelu)

            for b in range(BATCHES):
                act.wait_ge(shift_ready, b + 1)
                for g in (2 * b, 2 * b + 1):
                    for n in range(WIDE):
                        t = g * WIDE + n
                        last = nc.scalar.activation(fin[g][:, n * P:(n + 1) * P], bank[g][:, n * P:(n + 1) * P],
                                                    ACT.Identity, bias=cols(mean1, t, 1), scale=cols(rstd1, t, 1))
                    last.then_inc(fin_a, 1)

        @block.tensor
        def _(pe):
            mm = nc.tensor.matmul
            pe.wait_ge(wgt_loaded, 16)
            pe.wait_ge(silu_ready, 1)
            for n in range(2):
                mm(BB[:, n * BATCHES:(n + 1) * BATCHES], wgt("wmod")[:, n * P:(n + 1) * P],
                   silu[:, 2 * BATCHES:3 * BATCHES], start=True, stop=True, skip_group_check=True)\
                    .then_inc(mod_ready, 1)
            for b in range(BATCHES):
                mm(SC[b][:, :], cols(silu_bc, b), wgt("wmod")[:, 2 * P:6 * P],
                   start=True, stop=True).then_inc(mod_ready, 1)

            def transpose_in(u, p):
                need(pe, h0_ready, u + 1)
                need(pe, hT_ready, u)
                need(pe, qk_ready, u)
                nc.tensor.transpose(TB, h0[p][:, :], const("ident")).then_inc(h0T_ready, 1)

            def project_qk(u, p):
                need(pe, hT_ready, u + 1)
                need(pe, qk_ready, u)
                if isinstance(u, int):
                    need(pe, gm_read, (u - 3) // TPB)
                mm(QB[:, 0:P], wgt("wqT"), hT[p][:, :], start=True, stop=True)
                mm(QB[:, P:2 * P], wgt("wkT"), hT[p][:, :], start=True, stop=True, skip_group_check=True)\
                    .then_inc(qk_ps, 1)

            def project_kv(u, p):
                need(pe, kvs_ready, u)
                need(pe, um_ready, u)
                mm(KB[:, 0:2 * P], hT[p][:, :], WGT[:, weight_at["wvT"][0]:weight_at["wkT2"][1]],
                   start=True, stop=True, skip_group_check=True).then_inc(kv_ready, 1)

            def scores(t, p):
                need(pe, qm_ready, t + 1)
                q = Qm[p][:, :].rearrange("p (h i) -> p h i", i=P)
                for s in range(2):
                    if s == 1:
                        need(pe, qm2_ready, t + 1)
                    need(pe, p_ready, 2 * (t - 2) + s + 1)
                    for c in range(CPT):
                        at = slice(c * C, (c + 1) * C)
                        last = mm(SC[2 * p + s][at, :], QK[p][:, P + c * C:P + (c + 1) * C],
                                  q[:, s * HALF:(s + 1) * HALF, at], start=True, stop=True)
                    last.then_inc(sc_ready, 1)

            def state_update(t, p):
                need(pe, kvs_ready, t + 1)
                need(pe, um_ready, t)
                values = V[p][:, :].rearrange("p (h c) -> p h c", c=LANE)
                for c in range(CPT):
                    last = mm(KB[:, (2 + c) * P:(3 + c) * P], Kd[p][:, :], values[:, :, 32 * c:32 * c + DH],
                              start=True, stop=True, skip_group_check=True)
                last.then_inc(u_ready, 1)

            def outputs(t, p):
                need(pe, YT_ready, t)
                need(pe, qd_ready, t + 1)
                need(pe, s_ready, 2 * t + 1)
                out_at = lambda g: (slice(64 * (g % 2), 64 * (g % 2 + 1)), slice(g // 2 * C, (g // 2 + 1) * C))
                for s in range(2):
                    for c in range(CPT):
                        for g in (2 * s, 2 * s + 1):
                            rows, at = out_at(g)
                            mm(YB[rows, at], STATE[2 * p + c][:, 64 * g:64 * (g + 1)], Qd[p][:, c * C:(c + 1) * C],
                               start=(c == 0), stop=False, skip_group_check=True)
                    need(pe, p_ready, 2 * t + s + 1)
                    for a in range(HPG):
                        for g in (2 * s, 2 * s + 1):
                            rows, at = out_at(g)
                            col, h = g * HPG * LANE + 64 * a, g * HPG + a
                            last = mm(YB[rows, at], V[p][:, col:col + 64], PR[p][:, h * C:(h + 1) * C],
                                      start=False, stop=(a == HPG - 1), skip_group_check=True)
                last.then_inc(y_ready, 1)

            def step(t, p):
                if not last_tile(t):
                    project_qk(t + 1, 1 - p)
                state_update(t, p)
                scores(t, p)
                if not last_tile(t):
                    project_kv(t + 1, 1 - p)
                stages(b_first, t)
                if not near_end(t):
                    transpose_in(t + 2, p)
                stages(b_stage, t)
                outputs(t, p)

            def attend(b, p):
                g = 2 * b + p
                pe.wait_ge(yn_ready, g + 1)
                if p == 0 and b == BATCHES - 1:
                    pe.wait_ge(p_ready, 2 * TILES)
                elif p == 0:
                    need(pe, rank_read, b)
                else:
                    pe.wait_ge(x2_ready, g)
                for n in range(WIDE):
                    last = mm(SIDE[b][:, n * P:(n + 1) * P], yn[p][:, n * P:(n + 1) * P], cols(WOG, b), start=True,
                              stop=True, skip_group_check=True)
                last.then_inc(att_ready, 1)

            def h2_transpose(b, p):
                g = 2 * b + p
                pe.wait_ge(h2_ready, g + 1)
                if p == 0:
                    pe.wait_ge(x2_ready, g + 2)
                else:
                    pe.wait_ge(h2t_ready, g)
                for n in range(WIDE):
                    at = slice(n * P, (n + 1) * P)
                    last = nc.tensor.transpose(SIDE[b][:, at], h2[p][:, at], const("ident"))
                last.then_inc(h2T_ready, 1)

            def b_first(b, s):
                if s == 1:
                    pe.wait_ge(gmean_ready, b + 1)
                    pe.wait_ge(qk_ready, min(TPB * (b + 1) + 3, TILES))
                    mm(GM, const("head_mean"), gn[:, 2 * b:2 * b + 2], start=True, stop=True, skip_group_check=True)\
                        .then_inc(gm_ready, 1)

            def b_stage(b, s):
                if s in (4, 5):
                    attend(b, s - 4)
                if s in (7, 8):
                    h2_transpose(b, s - 7)
                if s == 9:
                    pe.wait_ge(h2t_ready, 2 * b + 2)
                    for t in range(TPB):
                        at = t % WIDE * P
                        last = mm(SIDE[b][:, t * EXPERTS:(t + 1) * EXPERTS], h2t[t // WIDE][:, at:at + P], wgt("rwT"),
                                  start=True, stop=True, skip_group_check=True)
                    last.then_inc(lg_ready, 1)
                if s == 11:
                    pe.wait_ge(chosen_ready, b + 1)
                    need(pe, total_ready, b)
                    mm(SIDE[b][:, 0:BE], const("before"), CHOSEN[0][:, BE:], start=True, stop=False)
                    mm(SIDE[b][:, 0:BE], const("ones"), CHOSEN[3][:, BE - EXPERTS:2 * BE - EXPERTS], start=False, stop=False)
                    mm(SIDE[b][:, 0:BE], const("ones"), CHOSEN_BEFORE[:, :].unsqueeze(1).broadcast_to((P, TPB, EXPERTS)),
                       start=False, stop=True).then_inc(rank_ready, 1)

            pe.wait_ge(const_loaded, 16)
            pe.wait_ge(mod_read, 2)
            transpose_in(0, 0)
            project_qk(0, 0)
            project_kv(0, 0)
            transpose_in(1, 1)
            pe.wait_ge(mod_read, 2 + BATCHES)
            pe.wait_ge(pool_step, 15)
            phases_a_b(pe, step, None)
            remaining_stages(b_first, b_stage)
            pe.wait_ge(total_ready, BATCHES)
            mm(bank[6][:, 0:EXPERTS], const("ones"), CHOSEN_BEFORE[:, :], start=True, stop=True)\
                .then_inc(count_ready, 1)

            pe.wait_ge(plan_ready, 3)

            def transpose_rows(r):
                for n in range(NS):
                    last = nc.tensor.transpose(bank[4 + r % 2][:, n * P:(n + 1) * P], IN[r][:, n * ROW:n * ROW + P],
                                               const("ident"))
                last.then_inc(inT_ps, 1)

            def expert_step(i, r):
                p = r % 2
                for f in range(FC):
                    if f == 0:
                        need(pe, w1_lo, i + 1)
                        need(pe, inT_ready, i + 1)
                    need(pe, hid_ready, (i - 1) * FC + f + 1)
                    at = slice(f * P, (f + 1) * P)
                    mm(bank[f][:, 0:SLOTS], W1_HI[p][:, at], ROW_HI[p][:, :], start=True, stop=False)
                    mm(bank[f][:, 0:SLOTS], W1_HI[p][:, at], ROW_LO[p][:, :], start=False, stop=False)
                    mm(bank[f][:, 0:SLOTS], W1_LO[p][:, at], ROW_HI[p][:, :], start=False, stop=True)\
                        .then_inc(hid_ps, 1)

            def second_layer(i, r):
                p = r % 2
                need(pe, res_ready, i - 1)
                for n in range(NS):
                    for f in range(FC):
                        if n == 0:
                            need(pe, hid_ready, i * FC + f + 1)
                        last = mm(bank[6 + p][:, n * P:(n + 1) * P], HID[f][:, n * P:(n + 1) * P],
                                  EW[r][:, FF + f * P:FF + (f + 1) * P], start=(f == 0), stop=(f == FC - 1),
                                  skip_group_check=True)
                last.then_inc(moe_ready, 1)

            def loaded(s, r, turn):
                pe.wait_ge(s[r], 16 * (turn + 1))

            def ring_round(turn, last):
                size = LAST_ROUND if last else RING
                for r in range(size):
                    i = RING * turn + r
                    loaded(ew_loaded, r, turn)
                    expert_step(i, r)
                    if not (last and r == size - 1):
                        rn = (r + 1) % RING
                        loaded(in_loaded, rn, turn + (r == RING - 1))
                        transpose_rows(rn)
                    second_layer(i, r)

            loaded(in_loaded, 0, 0)
            transpose_rows(0)
            ring_round(0, False)
            with pe.Fori(1, ROUNDS - 1) as turn:
                ring_round(turn, False)
            ring_round(ROUNDS - 1, True)

            pe.wait_ge(sum_ready, STEPS)
            for g in range(TILES // WIDE):
                rows = ROWS[0][:, g * WIDE * ROW:(g + 1) * WIDE * ROW].rearrange("p (n d) -> p n d", d=ROW)
                mm(bank[g][:, :], const("ident"), rows[:, :, 0:P], start=True, stop=False)
            for g in range(TILES // WIDE):
                pe.wait_ge(back_loaded[g % 4], 16 * TOP_K * (g // 4 + 1))
                for k in range(TOP_K):
                    last = mm(bank[g][:, :], const("ident"), BACK[g % 4][:, k * WIDE * P:(k + 1) * WIDE * P],
                              start=False, stop=(k == TOP_K - 1))
                last.then_inc(sum_ps, 1)

        @block.vector
        def _(dve):
            v = nc.vector
            chain = [0]

            def link(ins):
                chain[0] += 1
                ins.then_inc(dve_chain, 1)
                dve.wait_ge(dve_chain, chain[0])

            def moments(stats, mean, variance, tmp, eps, sign=1.0):
                s = stats.rearrange("p (t s) -> p t s", s=6)
                link(v.tensor_tensor(tmp, s[:, :, 1], s[:, :, 4], ALU.subtract))
                link(v.tensor_tensor(mean, s[:, :, 1], s[:, :, 4], ALU.add))
                link(v.tensor_scalar(mean, mean, 0.5 * sign, None, ALU.mult))
                link(v.tensor_tensor(tmp, tmp, tmp, ALU.mult))
                link(v.tensor_tensor(variance, s[:, :, 2], s[:, :, 5], ALU.add))
                link(v.tensor_scalar(variance, variance, 1.0 / P, eps, ALU.mult, ALU.add))
                v.scalar_tensor_tensor(out=variance, in0=tmp, scalar=0.25, in1=variance, op0=ALU.mult,
                                       op1=ALU.add).then_inc(var_ready, 1)

            def per_batch(ap):
                return ap.unsqueeze(2).broadcast_to((P, BATCHES, TPB))

            dve.wait_ge(act_step, 1)
            link(v.tensor_scalar(silu[:, 0:BATCHES], silu[:, 0:BATCHES], 1.0, None, ALU.add))
            link(v.reciprocal(silu[:, BATCHES:2 * BATCHES], silu[:, 0:BATCHES]))
            link(v.tensor_tensor(silu[:, 2 * BATCHES:3 * BATCHES], silu[:, BATCHES:2 * BATCHES], wgt("cT"), ALU.mult))
            v.tensor_copy(silu_bc[:, :].rearrange("p (b m) -> p b m", b=BATCHES),
                          silu[:, 2 * BATCHES:3 * BATCHES].unsqueeze(2).broadcast_to((P, BATCHES, P)))\
             .then_inc(silu_ready, 1)

            def first_stats(b):
                dve.wait_ge(x_loaded[b], 16)
                for t in range(b * TPB, (b + 1) * TPB):
                    last = v.bn_stats(cols(stat, t, 6), cols(X, t))
                link(last)
                at = slice(b * TPB, (b + 1) * TPB)
                moments(stat[:, b * TPB * 6:(b + 1) * TPB * 6], mean1[:, at], var[:, at], half[:, at], EPS)

            first_stats(0)

            dve.wait_ge(mod_ready, 2)
            sa, ca = BB[:, 0:BATCHES], BB[:, BATCHES:2 * BATCHES]
            v.tensor_copy(shiftT[:, :].rearrange("p (b t) -> p b t", b=BATCHES), per_batch(sa)).then_inc(mod_read, 1)
            v.tensor_scalar(scaleT[:, :].rearrange("p (b t) -> p b t", b=BATCHES), per_batch(ca), 1.0, None,
                            ALU.add).then_inc(mod_read, 1)
            mod = MOD[:, :].rearrange("p (b k d) -> p b k d", b=BATCHES, k=4)
            three = lambda tensor: tensor[:, 0:BATCHES * P].rearrange("p (b d) -> p b d", b=BATCHES)
            spread = lambda ap: ap.unsqueeze(1).broadcast_to((P, BATCHES, P))

            def clamp_gate(k):
                g = mod[:, :, k, :]
                hi = gate[:, BATCHES * P:].rearrange("p (b d) -> p b d", b=BATCHES)
                link(v.scalar_tensor_tensor(out=hi, in0=g, scalar=-1.0, in1=g, op0=ALU.mult, op1=ALU.max))
                link(v.tensor_scalar(hi, hi, 0.25, None, ALU.max))
                link(v.tensor_scalar(three(gate), g, 0.0, 2.0, ALU.is_ge, ALU.mult))
                link(v.scalar_tensor_tensor(out=gate[:, 0:BATCHES * P], in0=gate[:, 0:BATCHES * P], scalar=-1.0,
                                            in1=gate[:, BATCHES * P:], op0=ALU.add, op1=ALU.mult))

            def early(n):
                if n + 1 < BATCHES:
                    first_stats(n + 1)
                    if n == 1:
                        dve.wait_ge(rstd_ready, 2)
                else:
                    dve.wait_ge(mod_read, 2 + BATCHES)
                    clamp_gate(0)
                    link(v.tensor_tensor(three(WOG), three(gate), spread(wgt("woT")), ALU.mult))
                    link(v.tensor_scalar(mod[:, :, 2, :], mod[:, :, 2, :], 1.0, None, ALU.add))
                    for k in range(TOP_K):
                        dst = ROWS[k][:, :].rearrange("p (t d) -> p t d", d=ROW)[:, :, P]
                        link(v.tensor_scalar(dst, const("token"), float(k * TOKENS), None, ALU.add))
                    dve.wait_ge(rstd_ready, BATCHES)

            def normalise(u, p):
                need(dve, h0T_ready, u - 1)
                v.tensor_scalar(h0[p][:, :], cols(X, u), cols(mean1, u, 1), cols(rstd1, u, 1), ALU.subtract,
                                ALU.mult).then_inc(h0_ready, 1)

            def keys_values(u, p):
                need(dve, y_ready, u - 1)
                need(dve, kv_ready, u + 1)
                for c in range(CPT):
                    rows = slice(c * C, (c + 1) * C)
                    v.tensor_copy(V[p][rows, :].rearrange("p (h c) -> p h c", c=LANE)[:, :, 32 * c:32 * c + DH],
                                  KB[rows, 0:P].rearrange("p (h d) -> p h d", d=DH))
                v.tensor_tensor(Kd[p][:, :], KB[:, P:2 * P], const("kdec"), ALU.mult).then_inc(kvs_ready, 1)

            def mask(t, p):
                for s in range(2):
                    need(dve, sc_ready, 2 * t + s + 1)
                    if s == 0:
                        need(dve, y_ready, t - 1)
                    at = slice(s * HALF * C, (s + 1) * HALF * C)
                    v.tensor_tensor(PR[p][:, at], SC[2 * p + s][:, :], const("decay")[:, at], ALU.mult)\
                     .then_inc(p_ready, 1)

            def state(t, p):
                need(dve, u_ready, t + 1)
                need(dve, s_ready, 2 * t)
                v.tensor_tensor(UM[:, :].rearrange("p (c d) -> p c d", c=CPT),
                                KB[:, 2 * P:4 * P].rearrange("p (c d) -> p c d", c=CPT),
                                const("same_head").unsqueeze(1).broadcast_to((P, CPT, P)), ALU.mult)\
                 .then_inc(um_ready, 1)
                for c in range(CPT):
                    if c == 0:
                        need(dve, um_ready, t + 1)
                        need(dve, y_ready, t)
                    else:
                        need(dve, s_ready, 2 * t + 1)
                    view = lambda n: STATE[n][:, :].rearrange("p (g d) -> p g d", d=64)[:, :, 32 * (n % 2):32 * (n % 2 + 1)]
                    v.scalar_tensor_tensor(out=view((2 * p + c + 1) % 4), in0=view(2 * p + c),
                                           scalar=cols(const("carry"), 2 * t + c, 1),
                                           in1=UM[:, c * P:(c + 1) * P].rearrange("p (g d) -> p g d", d=32),
                                           op0=ALU.mult, op1=ALU.add).then_inc(s_ready, 1)

            def y_stats(t):
                v.bn_stats(cols(ystat, t, 6), cols(YT, t)).then_inc(ystat_ready, 1)

            def step(t, p):
                if not near_end(t):
                    normalise(t + 2, p)
                state(t, p)
                need(dve, YT_ready, t)
                mask(t, p)
                if not last_tile(t):
                    keys_values(t + 1, 1 - p)
                if not (isinstance(t, int) and t == 0):
                    y_stats(t - 1)

            def head_moments(b):
                if b == BATCHES - 1:
                    dve.wait_ge(YT_ready, TILES)
                    y_stats(TILES - 1)
                dve.wait_ge(ystat_ready, (b + 1) * TPB)
                ys = ystat[:, b * TPB * 6:(b + 1) * TPB * 6].rearrange("p (n s) -> p n s", s=3)
                mu, m2 = ys[:, :, 1], ys[:, :, 2]
                mean_c, square_c = gn[:, 2 * b:2 * b + 1], gn[:, 2 * b + 1:2 * b + 2]
                sq = stat[:, 0:2 * TPB]
                v.tensor_reduce(mean_c, mu, AX.X, ALU.add)
                link(v.tensor_tensor(sq, mu, mu, ALU.mult))
                v.tensor_scalar(mean_c, mean_c, 1.0 / (2 * TPB), None, ALU.mult)
                link(v.scalar_tensor_tensor(out=sq, in0=sq, scalar=P / 2.0, in1=m2, op0=ALU.mult, op1=ALU.add))
                link(v.tensor_reduce(square_c, sq, AX.X, ALU.add))
                v.tensor_scalar(square_c, square_c, 1.0 / SEQ, None, ALU.mult).then_inc(gmean_ready, 1)

            mean_h, square_h, var_h, rstd_h = [lambda b, n=n: gsc[:, 4 * b + n:4 * b + n + 1] for n in range(4)]

            def head_variance(b):
                dve.wait_ge(gm_read, b + 1)
                link(v.tensor_tensor(var_h(b), mean_h(b), mean_h(b), ALU.mult))
                link(v.tensor_tensor(var_h(b), square_h(b), var_h(b), ALU.subtract))
                v.tensor_scalar(var_h(b), var_h(b), EPS, None, ALU.add).then_inc(var_ready, 1)

            def norm_affine(b):
                dve.wait_ge(rstd_ready, BATCHES + 2 * b + 1)
                link(v.tensor_scalar(rstd_h(b), rstd_h(b), wgt("gn_w"), None, ALU.mult))
                link(v.tensor_tensor(mean_h(b), mean_h(b), rstd_h(b), ALU.mult))
                v.tensor_scalar(mean_h(b), mean_h(b), -1.0, wgt("gn_b"), ALU.mult, ALU.add).then_inc(gn_ready, 1)

            def residual(b, p):
                g = 2 * b + p
                dve.wait_ge(att_ready, g + 1)
                x4 = X[:, g * WIDE * P:(g + 1) * WIDE * P]
                v.tensor_tensor(x4, SIDE[b][:, :], x4, ALU.add).then_inc(x2_ready, 1)
                dve.wait_ge(x2_ready, g + 1)
                for n in range(WIDE):
                    t = g * WIDE + n
                    last = v.bn_stats(cols(xstat, t, 6), cols(X, t))
                if p == 1:
                    link(last)
                    at = slice(b * TPB, (b + 1) * TPB)
                    moments(xstat[:, b * TPB * 6:(b + 1) * TPB * 6], mean2[:, at], var[:, at], half[:, at], EPS,
                            sign=-1.0)

            over = lambda ap: ap.unsqueeze(1).broadcast_to((P, TPB, EXPERTS))
            te = lambda n: route[:, n * BE:(n + 1) * BE].rearrange("p (t e) -> p t e", e=EXPERTS)
            wide = lambda ap: ap.unsqueeze(2).broadcast_to((P, TPB, EXPERTS))
            per_tile = lambda n: topv[:, n * TPB:(n + 1) * TPB]
            four = lambda ap: ap.rearrange("p (n d) -> p n d", d=P)
            all4 = lambda ap: ap.unsqueeze(1).broadcast_to((P, WIDE, P))

            def hidden(b, p):
                g = 2 * b + p
                dve.wait_ge(n2_ready, g + 1)
                v.tensor_tensor(four(hn[p][:, :]), four(hn[p][:, :]), all4(cols(MOD, 4 * b + 2)), ALU.mult)\
                 .then_inc(m2_ready, 1)
                dve.wait_ge(m2_ready, g + 1)
                need(dve, h2T_ready, g - 1)
                need(dve, row_ready, TOP_K * (g - 1))
                v.tensor_tensor(four(h2[p][:, :]), four(hn[p][:, :]), all4(cols(MOD, 4 * b + 1)), ALU.add)\
                 .then_inc(h2_ready, 1)

            def first_of_largest(logits, value, onehot):
                link(v.tensor_reduce(value, logits, AX.X, ALU.max))
                link(v.tensor_tensor(onehot, logits, wide(value), ALU.is_equal))
                link(v.tensor_tensor(onehot, onehot, over(const("rank")), ALU.mult))
                link(v.tensor_reduce(per_tile(2), onehot, AX.X, ALU.max))
                link(v.tensor_tensor(onehot, over(const("rank")), wide(per_tile(2)), ALU.is_equal))

            def first_choice(b):
                dve.wait_ge(lg_ready, b + 1)
                v.tensor_tensor(te(0), SIDE[b][:, 0:BE].rearrange("p (t e) -> p t e", e=EXPERTS), over(wgt("r_b")),
                                ALU.add).then_inc(lg_read, 1)
                dve.wait_ge(lg_read, b + 1)
                first_of_largest(te(0), per_tile(0), te(1))
                link(v.scalar_tensor_tensor(out=te(2), in0=te(1), scalar=-3.0e38, in1=te(0), op0=ALU.mult,
                                            op1=ALU.add))

            def second_choice(b):
                first_of_largest(te(2), per_tile(1), te(3))
                v.tensor_tensor(per_tile(2), per_tile(1), per_tile(0), ALU.subtract).then_inc(exp_in, 1)
                need(dve, rank_ready, b)
                link(v.tensor_tensor(CHOSEN[0][:, BE:], route[:, BE:2 * BE], route[:, 3 * BE:4 * BE], ALU.add))
                for n in range(3):
                    back = EXPERTS << n
                    ins = v.tensor_tensor(CHOSEN[n + 1][:, BE:], CHOSEN[n][:, BE:], CHOSEN[n][:, BE - back:2 * BE - back],
                                          ALU.add)
                    if n < 2:
                        link(ins)
                ins.then_inc(chosen_ready, 1)

            def weights_and_slots(b):
                weight = [ROWS[k][:, b * TPB * ROW:(b + 1) * TPB * ROW].rearrange("p (t d) -> p t d", d=ROW)[:, :, P + 1]
                          for k in range(TOP_K)]
                dve.wait_ge(rank_ready, b + 1)
                v.tensor_tensor(te(0), SIDE[b][:, 0:BE].rearrange("p (t e) -> p t e", e=EXPERTS),
                                over(const("region")), ALU.add).then_inc(rank_read, 1)
                dve.wait_ge(exp_out, b + 1)
                link(v.tensor_scalar(per_tile(2), per_tile(3), 1.0, None, ALU.add))
                dve.wait_ge(rank_read, b + 1)
                v.tensor_tensor(te(1), te(1), te(0), ALU.mult)
                v.tensor_tensor(te(3), te(3), te(0), ALU.mult)
                link(v.reciprocal(weight[0], per_tile(2)))
                v.tensor_reduce(slotf[:, 0:TPB], te(1), AX.X, ALU.add)
                v.tensor_reduce(slotf[:, TPB:], te(3), AX.X, ALU.add)
                link(v.tensor_tensor(weight[1], weight[0], per_tile(3), ALU.mult))
                v.tensor_copy(SLOT[:, b * TOP_K * TPB:(b + 1) * TOP_K * TPB], slotf[:, :]).then_inc(slot_ready, 1)
                v.tensor_tensor(CHOSEN_BEFORE[:, :], CHOSEN_BEFORE[:, :], CHOSEN[3][:, 2 * BE - EXPERTS:], ALU.add)\
                 .then_inc(total_ready, 1)

            def b_stage(b, s):
                work = {0: head_moments, 1: head_variance, 2: norm_affine, 9: first_choice, 10: second_choice,
                        11: weights_and_slots}
                if s in work:
                    work[s](b)
                if s in (4, 5):
                    residual(b, s - 4)
                if s in (6, 7):
                    hidden(b, s - 6)

            dve.wait_ge(rstd_ready, 1)
            dve.wait_ge(pool_step, 15)
            normalise(0, 0)
            normalise(1, 1)
            for b in range(BATCHES):
                dve.wait_ge(mod_ready, 3 + b)
                v.tensor_copy(MOD[:, b * 4 * P:(b + 1) * 4 * P], SC[b][:, :]).then_inc(mod_read, 1)
            keys_values(0, 0)
            dve.wait_ge(decay_loaded, 16)
            phases_a_b(dve, step, b_stage, early)

            dve.wait_ge(count_ready, 1)
            dve.wait_ge(plan_loaded, 16)
            at, work = 0, {}
            for name, n in [("count", EXPERTS), ("steps", EXPERTS), ("upto", EXPERTS), ("end", EXPERTS),
                            ("past", STEPS * EXPERTS), ("spent", STEPS * EXPERTS), ("expert", STEPS),
                            ("start", STEPS), ("used", STEPS), ("skip", STEPS), ("begun", EXPERTS * (TOKENS // SLOTS))]:
                work[name] = plan_w[:, at:at + n]
                at += n
            table = lambda name: PLAN[:, plan_at[name][0]:plan_at[name][1]]
            pairs = lambda ap, n: ap.rearrange("p (a b) -> p a b", b=n)
            per_row = lambda ap, n: ap.unsqueeze(2).broadcast_to((1, ap.shape[1], n))
            per_col = lambda ap, n: ap.unsqueeze(1).broadcast_to((1, n, ap.shape[1]))
            FS = TOKENS // SLOTS
            link(v.tensor_copy(work["count"], bank[6][0:1, 0:EXPERTS]))
            link(v.tensor_tensor(work["end"], work["count"], table("start"), ALU.add))
            v.tensor_copy(FILLED[:, :], work["end"]).then_inc(plan_ready, 1)
            link(v.tensor_tensor(pairs(work["begun"], FS), per_row(work["count"], FS), pairs(table("fill"), FS),
                                 ALU.is_gt))
            link(v.tensor_reduce(work["steps"], pairs(work["begun"], FS), AX.X, ALU.add))
            upto = work["past"][:, 0:EXPERTS * EXPERTS]
            link(v.tensor_tensor(pairs(upto, EXPERTS), pairs(table("upto"), EXPERTS), per_col(work["steps"], EXPERTS),
                                 ALU.mult))
            link(v.tensor_reduce(work["upto"], pairs(upto, EXPERTS), AX.X, ALU.add))
            link(v.tensor_tensor(pairs(work["past"], EXPERTS), pairs(table("step"), EXPERTS),
                                 per_col(work["upto"], STEPS), ALU.is_ge))
            link(v.tensor_tensor(pairs(work["spent"], EXPERTS), pairs(work["past"], EXPERTS),
                                 per_col(work["steps"], STEPS), ALU.mult))
            link(v.tensor_reduce(work["expert"], pairs(work["past"], EXPERTS), AX.X, ALU.add))
            link(v.tensor_reduce(work["skip"], pairs(work["spent"], EXPERTS), AX.X, ALU.add))
            link(v.tensor_tensor(work["start"], table("index"), work["skip"], ALU.subtract))
            link(v.tensor_scalar(work["used"], work["expert"], EXPERTS - 0.5, float(SLOTS), ALU.is_lt, ALU.mult))
            link(v.tensor_tensor(work["start"], work["start"], work["used"], ALU.mult))
            link(v.scalar_tensor_tensor(out=work["start"], in0=work["expert"], scalar=float(REGION), in1=work["start"],
                                        op0=ALU.mult, op1=ALU.add))
            link(v.tensor_scalar(work["expert"], work["expert"], float(EXPERTS - 1), None, ALU.min))
            v.tensor_copy(STEP_START[:, :], work["start"]).then_inc(plan_ready, 1)
            v.tensor_copy(STEP_EXPERT[:, :], work["expert"]).then_inc(plan_ready, 1)

            dve.wait_ge(plan_ready, 3)
            clamp_gate(3)
            link(v.tensor_tensor(three(LNW), three(gate), spread(wgt("ln_w")), ALU.mult))
            link(v.tensor_tensor(three(LNB), three(gate), spread(wgt("ln_b")), ALU.mult))
            y4 = YT[:, :].rearrange("p (b t d) -> p b t d", b=BATCHES, d=P)
            x4 = X[:, :].rearrange("p (b t d) -> p b t d", b=BATCHES, d=P)
            for b in range(BATCHES):
                link(v.tensor_tensor(y4[:, b], x4[:, b], cols(LNB, b).unsqueeze(1).broadcast_to((P, TPB, P)), ALU.add))

            def split_w1(i, r):
                need(dve, w1_hi, i + 1)
                v.tensor_tensor(W1_LO[r % 2], EW[r][:, 0:FF], W1_HI[r % 2].bitcast(F32), ALU.subtract)\
                 .then_inc(w1_lo, 1)

            def take_rows(i, r):
                p = r % 2
                need(dve, inT_ps, i + 1)
                need(dve, hid_ps, FC * (i - 1))
                v.tensor_copy(ROW_HI[p][:, :], bank[4 + p][:, 0:SLOTS]).then_inc(row_hi, 1)
                need(dve, row_hi, i + 1)
                v.tensor_tensor(ROW_LO[p][:, :], bank[4 + p][:, 0:SLOTS], ROW_HI[p][:, :].bitcast(F32), ALU.subtract)\
                 .then_inc(inT_ready, 1)

            def take_dest(i, r):
                p = r % 2
                need(dve, sent_back[p], (i - p) * 8 * NS)
                v.tensor_copy(DEST[p][:, :], IN[r][:, :].rearrange("p (n d) -> p n d", d=ROW)[:, :, P])\
                 .then_inc(dest_ready, 1)
                need(dve, moe_ready, i + 1)
                v.tensor_tensor(RES[p][:, :].rearrange("p (n d) -> p n d", d=P),
                                bank[6 + p][:, 0:SLOTS].rearrange("p (n d) -> p n d", d=P),
                                EW[r][:, FF + FC * P + FC:].unsqueeze(1).broadcast_to((P, NS, P)), ALU.add)\
                 .then_inc(sum_ready, 1)
                need(dve, sum_ready, i + 1)
                for n in range(NS):
                    w = n * ROW + P + 1
                    last = v.tensor_scalar(RES[p][:, n * P:(n + 1) * P], RES[p][:, n * P:(n + 1) * P],
                                           IN[r][:, w:w + 1], None, ALU.mult)
                last.then_inc(res_ready, 1)

            def c_step(i, r):
                if not (isinstance(i, int) and i == STEPS - 1):
                    split_w1(i + 1, (r + 1) % RING)
                    take_rows(i + 1, (r + 1) % RING)
                take_dest(i, r)

            split_w1(0, 0)
            take_rows(0, 0)
            expert_loop(dve, c_step)

            def sum_stats(g):
                dve.wait_ge(sum_ps, g + 1)
                for n in range(WIDE):
                    last = v.bn_stats(cols(fstat, g * WIDE + n, 6), bank[g][:, n * P:(n + 1) * P])
                return last

            def last_moments(b):
                at = slice(b * TPB, (b + 1) * TPB)
                moments(fstat[:, b * TPB * 6:(b + 1) * TPB * 6], mean1[:, at], var[:, at], half[:, at], EPS_FFN)

            def shift(b):
                at = slice(b * TPB, (b + 1) * TPB)
                dve.wait_ge(rstd_ready, 3 * BATCHES + b + 1)
                v.scalar_tensor_tensor(out=mean1[:, at], in0=mean1[:, at], scalar=-1.0, in1=rstd1[:, at],
                                       op0=ALU.mult, op1=ALU.mult).then_inc(shift_ready, 1)

            def scale(b):
                for g in (2 * b, 2 * b + 1):
                    dve.wait_ge(fin_a, g + 1)
                    v.tensor_tensor(four(fin[g]), four(fin[g]), all4(cols(LNW, b)), ALU.mult).then_inc(fin_b, 1)

            for b in range(BATCHES):
                sum_stats(2 * b)
                if b >= 1:
                    shift(b - 1)
                link(sum_stats(2 * b + 1))
                last_moments(b)
                if b >= 1:
                    scale(b - 1)
            shift(BATCHES - 1)
            scale(BATCHES - 1)
            for g in range(BY_POOL, TILES // WIDE):
                dve.wait_ge(fin_b, g + 1)
                v.tensor_tensor(fin[g], fin[g], YT[:, g * WIDE * P:(g + 1) * WIDE * P], ALU.add).then_inc(fin_late, 1)


def kernel(**inputs):
    import concourse.bacc as _bacc
    from concourse.bass_utils import run_bass_kernel_spmd as _run

    def arr(name):
        return np.ascontiguousarray(inputs[name])

    def rows(name):
        return np.tile(arr(name)[None, :], (P, 1))

    parts = {
        "wqT": arr("L0_attn_W_q").T, "wkT": arr("L0_attn_W_k").T, "wvT": arr("L0_attn_W_v").T,
        "wkT2": arr("L0_attn_W_k").T, "woT": arr("L0_attn_W_o").T, "wmod": arr("L0_wmod"), "cT": arr("L0_c").T,
        "gn_w": arr("L0_attn_gn_weight")[:, None], "gn_b": arr("L0_attn_gn_bias")[:, None],
        "rwT": arr("L0_ffn_router_w").T, "r_b": rows("L0_ffn_router_b"),
        "ln_w": rows("L0_ffn_ln_w"), "ln_b": rows("L0_ffn_ln_b"),
    }
    w1, w2, b1 = arr("L0_ffn_w1"), arr("L0_ffn_w2"), arr("L0_ffn_b1")
    experts = np.concatenate([
        w1.transpose(0, 2, 1),
        w2.transpose(0, 2, 1).reshape(EXPERTS, FC, P, P).transpose(0, 2, 1, 3).reshape(EXPERTS, P, FC * P),
        b1.reshape(EXPERTS, FC, P).transpose(0, 2, 1),
        np.broadcast_to(arr("L0_ffn_b2")[:, None, :], (EXPERTS, P, P))], axis=2)
    arrays = {
        "x": arr("L0_attn_x"),
        "weights": np.concatenate([parts[n] for n, _ in WEIGHTS], axis=1),
        "consts": np.concatenate(list(shape_constants().values()), axis=1),
        "experts": experts,
        "plan": np.concatenate(list(plan_tables().values()))[None, :],
    }
    arrays = {k: np.ascontiguousarray(a) for k, a in arrays.items()}
    nc = _bacc.Bacc("TRN2", target_bir_lowering=False, num_devices=1)
    args = [nc.dram_tensor(k, a.shape, mybir.dt.from_np(a.dtype), kind="ExternalInput").ap() for k, a in arrays.items()]
    args.append(nc.dram_tensor("out", arrays["x"].shape, F32, kind="ExternalOutput").ap())
    build(nc, *args)
    return _run(nc, [arrays], core_ids=[0]).results[0]["out"]
```
